# Optimizing a Trainium2 kernel written in Bass

```python
import numpy as np
import jax
import jax.numpy as jnp

def _softmax(x, axis=-1):
    return jax.nn.softmax(x, axis=axis)
def _gelu(x):
    return jax.nn.gelu(x, approximate=True)
def _silu(x):
    return jax.nn.silu(x)
def _sigmoid(x):
    return jax.nn.sigmoid(x)
def _layernorm(x, axis=-1, eps=1e-5):
    m = jnp.mean(x, axis=axis, keepdims=True)
    v = jnp.var(x, axis=axis, keepdims=True)
    return (x - m) / jnp.sqrt(v + eps)
def _scatter_add(tgt, idx, src, axis=0):
    return tgt.at[idx].add(src)
def _segment_sum(src, seg, n):
    return jax.ops.segment_sum(src, seg, n)

kernel_name = 'mk_adj_resnorm_d2_adj_128_c4228a'

def setup_inputs(seed: int = 0):
    np.random.seed(seed)
    _w = jnp.asarray
    def _rec_inputs():
        import jax
        import jax.numpy as jnp
        _gk = jax.random.key(seed)
        x = -0.000929 + 1 * jax.random.normal(jax.random.fold_in(_gk, 1), (8192, 128), jnp.float32)
        _w = (1.0 + jnp.arange(8192, dtype=jnp.float32)) ** -0.5
        _w = _w / _w.mean()
        _pij = jnp.clip(0.000976562 * _w[:, None] * _w[None, :], 0.0, 1.0)
        _a = jax.random.uniform(jax.random.fold_in(_gk, 2), (8192, 8192)) < _pij
        _a = jnp.logical_or(_a, jnp.eye(8192, dtype=bool))
        _af = _a.astype(jnp.float32)
        _af = _af * jax.random.uniform(jax.random.fold_in(_gk, 3), (8192, 8192), jnp.float32, 0.05, 1)
        adj = _af
        return x, adj
    x, adj = _rec_inputs()
    def _L0_gnn_setup():
        import jax, jax.numpy as jnp
        import numpy as np
        N = 8192
        H = 128
        key = jax.random.key(seed)
        k_x, k_A, k_W = jax.random.split(key, 3)
        x = jax.random.normal(k_x, (N, H), dtype=jnp.float32)
        A = jax.random.uniform(k_A, (N, N), dtype=jnp.float32)
        alpha = jnp.array([0.5], dtype=jnp.float32)
        bound = 1.0 / np.sqrt(H)
        W = jax.random.uniform(k_W, (H, H), dtype=jnp.float32, minval=-bound, maxval=bound)
        b = jnp.zeros((H,), dtype=jnp.float32)
        t = jnp.zeros((1,), dtype=jnp.float32)
        return {'t': t, 'x': x, 'A': A, 'alpha': alpha, 'W': W, 'b': b}
    _L0_gnn_all = _L0_gnn_setup()
    _L0_gnn_in = {k: v for k, v in _L0_gnn_all.items() if k in ('t', 'alpha', 'W', 'b', )}
    del _L0_gnn_all

    def _L1_gnn_setup():
        import jax, jax.numpy as jnp
        import numpy as np
        MIN_NORM = 1e-15
        PROJ_EPS = 1e-05
        C = 1.0

        def artanh(x):
            x = jnp.clip(x, -1.0 + 1e-07, 1.0 - 1e-07)
            return 0.5 * (jnp.log1p(x) - jnp.log1p(-x))

        def logmap0(p, c):
            sqrt_c = c ** 0.5
            norm = jnp.maximum(jnp.linalg.norm(p, axis=-1, keepdims=True), MIN_NORM)
            return p * (artanh(sqrt_c * norm) / (sqrt_c * norm))

        def expmap0(u, c):
            sqrt_c = c ** 0.5
            norm = jnp.maximum(jnp.linalg.norm(u, axis=-1, keepdims=True), MIN_NORM)
            return jnp.tanh(sqrt_c * norm) * u / (sqrt_c * norm)

        def proj(x, c):
            norm = jnp.maximum(jnp.linalg.norm(x, axis=-1, keepdims=True), MIN_NORM)
            maxnorm = (1.0 - PROJ_EPS) / c ** 0.5
            return jnp.where(norm > maxnorm, x / norm * maxnorm, x)

        def dense_att(x, adj, w, b):
            d = x.shape[-1]
            s_left = x @ w[:d]
            s_right = x @ w[d:]
            score = jax.nn.sigmoid(s_left[:, None] + s_right[None, :] + b[0])
            return adj * score
        key = jax.random.key(seed)
        k1, k2, k3, k4 = jax.random.split(key, 4)
        n, d = (8192, 128)
        x = jax.random.normal(k1, (n, d), jnp.float32) * 0.01
        adj = (jax.random.uniform(k2, (n, n), jnp.float32) < 0.005).astype(jnp.float32)
        std = 1.0 / np.sqrt(2 * d)
        w_par = jax.random.normal(k3, (2 * d,), jnp.float32) * std
        w_chi = jax.random.normal(k4, (2 * d,), jnp.float32) * std
        b_par = jnp.zeros((1,), jnp.float32)
        b_chi = jnp.zeros((1,), jnp.float32)
        return {'x': x, 'adj': adj, 'w_par': w_par, 'b_par': b_par, 'w_chi': w_chi, 'b_chi': b_chi}
    _L1_gnn_all = _L1_gnn_setup()
    _L1_gnn_in = {k: v for k, v in _L1_gnn_all.items() if k in ('w_par', 'b_par', 'w_chi', 'b_chi', )}
    del _L1_gnn_all

    return {
        "x": x,
        "adj": adj,
        "L0_gnn_t": _L0_gnn_in["t"],
        "L0_gnn_alpha": _L0_gnn_in["alpha"],
        "L0_gnn_W": _L0_gnn_in["W"],
        "L0_gnn_b": _L0_gnn_in["b"],
        "L1_gnn_w_par": _L1_gnn_in["w_par"],
        "L1_gnn_b_par": _L1_gnn_in["b_par"],
        "L1_gnn_w_chi": _L1_gnn_in["w_chi"],
        "L1_gnn_b_chi": _L1_gnn_in["b_chi"],
    }

def reference(x, adj, L0_gnn_t, L0_gnn_alpha, L0_gnn_W, L0_gnn_b, L1_gnn_w_par, L1_gnn_b_par, L1_gnn_w_chi, L1_gnn_b_chi):
    import jax
    import jax.numpy as jnp
    def _L0_gnn_ref(t, x, A, alpha, W, b):
        import jax, jax.numpy as jnp
        import numpy as np
        N = 8192
        H = 128
        a = alpha[0]
        A_prime = a * A
        diag = jnp.diagonal(A_prime) + (1.0 - a)
        A_prime = A_prime.at[jnp.arange(N), jnp.arange(N)].set(diag)
        out_degree = A_prime.sum(axis=1)
        inv_deg = jnp.where(out_degree == 0.0, 0.0, 1.0 / out_degree)
        x = inv_deg[:, None] * A_prime @ x
        x = x @ W.T + b
        return jax.nn.relu(x)

    def _L1_gnn_ref(x, adj, w_par, b_par, w_chi, b_chi):
        import jax, jax.numpy as jnp
        import numpy as np
        MIN_NORM = 1e-15
        PROJ_EPS = 1e-05
        C = 1.0

        def artanh(x):
            x = jnp.clip(x, -1.0 + 1e-07, 1.0 - 1e-07)
            return 0.5 * (jnp.log1p(x) - jnp.log1p(-x))

        def logmap0(p, c):
            sqrt_c = c ** 0.5
            norm = jnp.maximum(jnp.linalg.norm(p, axis=-1, keepdims=True), MIN_NORM)
            return p * (artanh(sqrt_c * norm) / (sqrt_c * norm))

        def expmap0(u, c):
            sqrt_c = c ** 0.5
            norm = jnp.maximum(jnp.linalg.norm(u, axis=-1, keepdims=True), MIN_NORM)
            return jnp.tanh(sqrt_c * norm) * u / (sqrt_c * norm)

        def proj(x, c):
            norm = jnp.maximum(jnp.linalg.norm(x, axis=-1, keepdims=True), MIN_NORM)
            maxnorm = (1.0 - PROJ_EPS) / c ** 0.5
            return jnp.where(norm > maxnorm, x / norm * maxnorm, x)

        def dense_att(x, adj, w, b):
            d = x.shape[-1]
            s_left = x @ w[:d]
            s_right = x @ w[d:]
            score = jax.nn.sigmoid(s_left[:, None] + s_right[None, :] + b[0])
            return adj * score
        x_tangent = logmap0(x, C)
        adj_att_par = dense_att(x_tangent, adj, w_par, b_par)
        adj_att_chi = dense_att(x_tangent, adj.T, w_chi, b_chi)
        support_t = adj_att_chi @ x_tangent + adj_att_par @ x_tangent
        return proj(expmap0(support_t, C), C)

    x = _layernorm(x + _L0_gnn_ref(L0_gnn_t, x, adj, L0_gnn_alpha, L0_gnn_W, L0_gnn_b), axis=-1)
    x = _layernorm(x + _L1_gnn_ref(x, adj, L1_gnn_w_par, L1_gnn_b_par, L1_gnn_w_chi, L1_gnn_b_chi), axis=-1)
    return x


_drawn_inputs = setup_inputs


def setup_inputs(seed=0):
    import zlib

    import numpy as np

    out = dict(_drawn_inputs(seed))
    spreads = {'L0_gnn_b': (0.0, 0.1)}
    factors = {'L1_gnn_w_par': 3.801, 'L1_gnn_w_chi': 4.306}
    for name, (base, spread) in spreads.items():
        noise = np.random.default_rng([zlib.crc32(name.encode()), seed]).standard_normal(out[name].shape)
        drawn = base * np.exp(spread * noise) if base else spread * noise
        out[name] = jnp.asarray(drawn.astype(out[name].dtype))
    for name, factor in factors.items():
        out[name] = (out[name] * factor).astype(out[name].dtype)
    return out
```

```python
from contextlib import ExitStack

import concourse.bass as bass
from concourse import mybir


F32 = mybir.dt.float32
ALU = mybir.AluOpType
ACT = mybir.ActivationFunctionType
ds = bass.ds

N = 8192
P = 128
D = 128
BP = 1024
NPAN = N // BP
TPP = BP // P
BANK = 512

NQ = 4
QC = N // NQ
BPQ = QC // BP
SLOTS = 4
TRIPS = N // (2 * P * SLOTS)
GC = 256
GT = GC // P
GPQ = QC // GC
NG = N // GC

CHUNKS = 4
CH = 2 * BP
UNITS = TPP
PHASES = 8
UPI = UNITS * PHASES
PSIG, CSIG, TBUF = 4, 2, 2
STEPS_PER_TRIP = 20
LN_EPS = 1e-5
MIN_NORM = 1e-15
CLIP = 1.0 - 1e-7
MAXNORM = 1.0 - 1e-5

NAT, TRN, DIST, TO_J, OUT = range(5)
PH = [
    (0, 0, 0, False, 1),
    (2, 1, 1, False, 0), (1, 2, 1, True, 1),
    (4, 3, 2, False, 0), (3, 4, 2, True, 1),
    (6, 5, 3, False, 0), (5, 6, 3, True, 1),
    (8, 7, 4, False, 0),
]
NBLK = 9
EVACS = 5


def adj_resnorm_kernel(nc, x_g, xT, g_blk, WT, b_row, alpha, w_par, b_par, w_chi, b_chi, out):
    with ExitStack() as ctx:
        def sb(name, shape):
            return ctx.enter_context(nc.sbuf_tensor(name, shape, F32))

        def sem(name):
            return ctx.enter_context(nc.semaphore(name))

        ring = sb("ring", [P, 3 * CHUNKS * CH])
        acc = sb("acc", [P, N])
        psig = sb("psig", [P, 4, BP])
        csig = sb("csig", [P, 2, BP])
        lI = sb("lI", [P, 2, 2, BP])
        lJ = sb("lJ", [P, 2, BP])
        xtI = sb("xtI", [P, TPP * D])
        xtJ = sb("xtJ", [P, TPP * D])
        prcr = sb("prcr", [P, N // P * 2])
        ones = sb("ones", [P, P])
        ident = sb("ident", [P, P])
        WTs = sb("WTs", [P, D])
        wl = sb("wl", [P, 2])
        wr = sb("wr", [P, 2])
        bpc = sb("bpc", [P, 2])
        bpc2 = sb("bpc2", [P, 2 * GT])
        brow = sb("brow", [1, D])
        alph = sb("alph", [P, 1])
        oma = sb("oma", [P, 1])
        epsc = sb("epsc", [P, 1])
        mv = sb("mv", [P, GT, 2])
        bst = sb("bst", [P, GT, 6])
        small = sb("small", [P, 16, GT])
        (std, rstd, ss, nrm, nrm2, clp, om, rom, tt2, uu, lnu, fac, um1, zz, ums, l1p) = [small[:, k, :] for k in range(16)]
        fs = sb("fs", [P, 11, N // P])
        mvf = sb("mvf", [P, N // P, 2])
        bstf = sb("bstf", [P, N // P, 6])

        accS = acc[:, 0:2 * QC].rearrange("p (q c) -> p q c", q=2)
        xg = acc[:, 2 * QC:2 * QC + 2 * BANK].rearrange("p (h c) -> p h c", h=2)
        yS = lI[:, :, :, :].rearrange("p a b c -> p a (b c)")
        stage = psig[:, :, :].rearrange("p a c -> p (a c)")
        dg, sf, rc, y_st, r_st, x1b, xt_st, xn, xTt, junk = [stage[:, k * GC:(k + 1) * GC] for k in range(10)]
        rows = stage[0:2, 10 * GC:11 * GC]
        g0 = [ring[:, s * 2 * CH:(s + 1) * 2 * CH].rearrange("p (b t c) -> p b t c", b=BPQ, t=2) for s in range(SLOTS)]

        uN = ring[:, 0:N]
        x1f = ring[:, N:2 * N]
        res_o = ring[:, 2 * N:3 * N]

        ps = [ctx.enter_context(nc.psum_tensor(f"ps{k}", [P, QC], F32)) for k in range(2)]
        TP = [ps[0][:, 0:BP], ps[0][:, BP:2 * BP]]
        OUTP = [ps[1][:, 0:BP], ps[1][:, BP:2 * BP]]

        x1_d = nc.dram_tensor("x1_d", [NG, P, GC], F32)
        xt_d = nc.dram_tensor("xt_d", [NG, P, GC], F32)
        plcl_d = nc.dram_tensor("plcl_d", [2, N], F32)

        const_in = sem("const_in")
        ident_ready = sem("ident_ready")
        oma_ready = sem("oma_ready")
        bpc2_ready = sem("bpc2_ready")
        g_in = [sem(f"g_in{s}") for s in range(SLOTS)]
        xg_in = [sem(f"xg_in{h}") for h in range(2)]
        pe_slots = sem("pe_slots")
        acc_step = sem("acc_step")
        acc_zeroed = sem("acc_zeroed")
        xT_in = sem("xT_in")
        xTs_scaled = sem("xTs_scaled")
        y_evac = sem("y_evac")
        deg_ready = sem("deg_ready")
        dve_step = sem("dve_step")
        y_ready = sem("y_ready")
        h_ready = sem("h_ready")
        xn_in = sem("xn_in")
        var_ready = sem("var_ready")
        std_ready = sem("std_ready")
        x1_ready = sem("x1_ready")
        x1_out = sem("x1_out")
        ss_ready = sem("ss_ready")
        nrm_ready = sem("nrm_ready")
        u_ready = sem("u_ready")
        ln_ready = sem("ln_ready")
        fac_ready = sem("fac_ready")
        xt_ready = sem("xt_ready")
        xt_out = sem("xt_out")
        xTp_ready = sem("xTp_ready")
        xTt_ready = sem("xTt_ready")
        proj_ready = sem("proj_ready")
        rows_ready = sem("rows_ready")
        rows_out = sem("rows_out")
        prcr_ready = sem("prcr_ready")

        c_in = [sem(f"c_in{k}") for k in range(3 * CHUNKS)]
        lI_in = sem("lI_in")
        lJ_in = sem("lJ_in")
        xtI_in = sem("xtI_in")
        xtJ_in = sem("xtJ_in")
        p_ready = sem("p_ready")
        c_ready = sem("c_ready")
        t_ready = sem("t_ready")
        nat_ready = sem("nat_ready")
        psig_free = sem("psig_free")
        csig_free = sem("csig_free")
        kt_ready = sem("kt_ready")
        sup_zeroed = sem("sup_zeroed")
        evac_done = sem("evac_done")

        x1f_in = [sem(f"x1f_in{h}") for h in range(4)]
        uT_ready = sem("uT_ready")
        u_copied = sem("u_copied")
        u_sumsq = sem("u_sumsq")
        f_step = sem("f_step")
        f_act = sem("f_act")
        fvar_ready = sem("fvar_ready")
        o_ready = sem("o_ready")
        out_done = sem("out_done")

        N_CONST = 9

        def constant_wait(eng):
            eng.wait_ge(const_in, 16 * N_CONST)

        def peeled(q):
            return 2 if q == 1 else 1

        block = ctx.enter_context(nc.Block())

        @block.sync
        def _(sp):
            for dst, src in (
                (WTs[:, :], WT), (brow[:, :], b_row.rearrange("(a d) -> a d", a=1)),
                (alph[:, :], alpha.rearrange("(a d) -> a d", a=1).to_broadcast([P, 1])),
                (bpc[:, 0:1], b_par.rearrange("(a d) -> a d", a=1).to_broadcast([P, 1])),
                (bpc[:, 1:2], b_chi.rearrange("(a d) -> a d", a=1).to_broadcast([P, 1])),
                (wl[:, 0:1], w_par[0:D].rearrange("(d a) -> d a", a=1)),
                (wl[:, 1:2], w_chi[0:D].rearrange("(d a) -> d a", a=1)),
                (wr[:, 0:1], w_par[D:2 * D].rearrange("(d a) -> d a", a=1)),
                (wr[:, 1:2], w_chi[D:2 * D].rearrange("(d a) -> d a", a=1)),
            ):
                sp.dma_start(dst, src).then_inc(const_in, 16)

            def load_trip(q, t, first=False):
                n = q * TRIPS + t
                for s in range(SLOTS):
                    if s % 2 == 0:
                        if not first:
                            used = sp.lower_val(n * SLOTS - SLOTS + s + 2)
                            constant_wait(sp)
                            sp.wait_ge(pe_slots, used)
                        sp.dma_start(xg[:, s // 2, :].rearrange("p (g c) -> p g c", g=2),
                                     x_g[ds(t * 4 + s, 2)].rearrange("g p c -> p g c")).then_inc(xg_in[s // 2], 16)
                    if not first:
                        used = sp.lower_val(n * SLOTS - SLOTS + s + 1)
                        added = sp.lower_val((n * SLOTS - SLOTS + s + 1) * 2)
                        constant_wait(sp)
                        sp.wait_ge(pe_slots, used)
                        sp.wait_ge(acc_step, added)
                    for b in range(BPQ):
                        sp.dma_start(g0[s][:, b], g_blk[t, q * BPQ + b, s * 2 * P:(s + 1) * 2 * P, :]
                                     .rearrange("(t p) c -> p t c", p=P)).then_inc(g_in[s], 16)

            for q in range(NQ):
                if q == 0:
                    load_trip(0, 0, first=True)
                with sp.Fori(1 if q == 0 else 0, TRIPS) as t:
                    load_trip(q, t)

            def users(blk):
                return [([k for k in range(PHASES) if PH[k][use] == blk] or [None])[0] for use in (TRN, NAT)]

            def load_block(it, b, prev=None, prev_it=None):
                other = (it + (b + 1) // 2) % NPAN
                src = g_blk[it, other] if b % 2 == 1 else g_blk[other, it]
                for c in range(CHUNKS):
                    if prev is not None:
                        trn, nat = users(prev)
                        turned = None if trn is None else sp.lower_val(prev_it * UPI + (trn + 1) * UNITS)
                        used = None if nat is None else sp.lower_val(prev_it * UPI + nat * UNITS + 2 * c + 2)
                        constant_wait(sp)
                        if trn is not None:
                            sp.wait_ge(t_ready, turned)
                        if nat is not None:
                            sp.wait_ge(nat_ready, used)
                    k = (b % 3) * CHUNKS + c
                    sp.dma_start(ring[:, k * CH:(k + 1) * CH].rearrange("p (t c) -> p t c", t=2),
                                 src[c * 2 * P:(c + 1) * 2 * P, :].rearrange("(t p) c -> p t c", p=P)) \
                        .then_inc(c_in[k], 16)

            def load_xt(dst, panel, done):
                sp.dma_start(dst[:, :].rearrange("p (g c) -> p g c", g=BP // GC),
                             xt_d[ds(panel * (BP // GC), BP // GC)].rearrange("g p c -> p g c")).then_inc(done, 16)

            def load_l(dst, panel, done):
                for r in range(2):
                    sp.dma_start(dst[:, r, :], plcl_d[r:r + 1, ds(panel * BP, BP)].to_broadcast([P, BP])) \
                        .then_inc(done, 16)

            def phase_end(it, ph):
                return sp.lower_val(it * UPI + (ph + 1) * UNITS + PSIG)

            sp.wait_ge(pe_slots, NQ * TRIPS * SLOTS)
            sp.wait_ge(acc_step, NQ * TRIPS * SLOTS * 2)
            load_block(0, 0)
            load_block(0, 2)
            load_block(0, 1)
            sp.wait_ge(xt_out, 16 * NG)
            sp.wait_ge(rows_out, 16 * NG)
            sp.wait_ge(y_ready, NG)
            load_xt(xtI, 0, xtI_in)
            load_l(lI[:, 0], 0, lI_in)
            load_xt(xtJ, 1, xtJ_in)
            load_l(lJ, 1, lJ_in)

            def iteration(it, last):
                for d in range(2, 5):
                    load_block(it, 2 * d - 1, 2 * d - 4, it)
                    used = phase_end(it, 2 * d - 3)
                    constant_wait(sp)
                    sp.wait_ge(psig_free, used)
                    load_xt(xtJ, (it + d) % NPAN, xtJ_in)
                    load_block(it, 2 * d, 2 * d - 3, it)
                    if d < 4:
                        used = sp.lower_val(it * UPI + (2 * d - 1) * UNITS)
                        constant_wait(sp)
                        sp.wait_ge(c_ready, used)
                        sp.wait_ge(p_ready, used)
                        load_l(lJ, (it + d) % NPAN, lJ_in)
                if last:
                    return
                load_block(it + 1, 0, 6, it)
                used = phase_end(it, 6)
                constant_wait(sp)
                sp.wait_ge(psig_free, used)
                load_xt(xtI, it + 1, xtI_in)
                load_l(lI[:, (it + 1) % 2], it + 1, lI_in)
                used = sp.lower_val(it * UPI + 7 * UNITS)
                constant_wait(sp)
                sp.wait_ge(c_ready, used)
                sp.wait_ge(p_ready, used)
                load_l(lJ, (it + 2) % NPAN, lJ_in)
                load_block(it + 1, 2, 8, it)
                load_block(it + 1, 1, 7, it)
                used = phase_end(it, 7)
                constant_wait(sp)
                sp.wait_ge(psig_free, used)
                load_xt(xtJ, (it + 2) % NPAN, xtJ_in)

            with sp.Fori(0, NPAN - 1) as it:
                iteration(it, False)
            iteration(NPAN - 1, True)

            sp.wait_ge(x1_out, 16 * NG)
            sp.wait_ge(t_ready, NPAN * UPI)
            sp.wait_ge(nat_ready, NPAN * UPI)
            for h in range(4):
                g = NG // 4
                sp.dma_start(x1f[:, h * g * GC:(h + 1) * g * GC].rearrange("p (g c) -> p g c", g=g),
                             x1_d[h * g:(h + 1) * g].rearrange("g p c -> p g c")).then_inc(x1f_in[h], 16)
            for p in range(NPAN):
                sp.wait_ge(o_ready, p + 1)
                sp.dma_start(out[p * BP:(p + 1) * BP, :].rearrange("(t p) d -> p t d", p=P),
                             res_o[:, p * BP:(p + 1) * BP].rearrange("p (t d) -> p t d", t=TPP)).then_inc(out_done, 16)
            sp.wait_ge(out_done, 16 * NPAN)

        @block.gpsimd
        def _(pool):
            pool.memset(ones[:, :], 1.0).then_inc(ident_ready, 1)
            pool.memset(epsc[:, :], LN_EPS).then_inc(ident_ready, 1)
            pool.memset(ident[:, :], 0.0).then_inc(ident_ready, 1)
            pool.wait_ge(ident_ready, 3)
            pool.affine_select(out=ident[:, :], in_=ident[:, :], compare_op=ALU.not_equal, fill=1.0, base=0,
                               pattern=[[-1, P]], channel_multiplier=1).then_inc(ident_ready, 1)
            pool.sem_inc(psig_free, PSIG)
            pool.sem_inc(csig_free, CSIG)
            pool.sem_inc(kt_ready, TBUF)
            pool.sem_inc(evac_done, 1)

            for q in range(NQ):
                if q >= 2:
                    pool.wait_ge(deg_ready, GPQ * (q - 1))
                pool.memset(accS[:, q % 2, :], 0.0).then_inc(acc_zeroed, 1)

            pool.wait_ge(deg_ready, NG)
            pool.wait_ge(pe_slots, NQ * TRIPS * SLOTS)
            pool.memset(acc[:, :], 0.0).then_inc(sup_zeroed, 1)

            with pool.Fori(0, NPAN) as it:
                for ph in range(PHASES):
                    blk = PH[ph][NAT]
                    for u in range(UNITS):
                        n = ph * UNITS + u
                        k = (blk % 3) * CHUNKS + u // 2
                        if u % 2 == 0:
                            pool.wait_ge(c_in[k], (it * 3 + blk // 3 + 1) * 16)
                        pool.wait_ge(p_ready, it * UPI + n + 1)
                        pool.tensor_tensor(out=psig[:, n % PSIG, :], in0=psig[:, n % PSIG, :],
                                           in1=ring[:, k * CH + (u % 2) * BP:k * CH + (u % 2 + 1) * BP],
                                           op=ALU.mult).then_inc(nat_ready, 1)

        @block.scalar
        def _(act):
            def load_xT(q):
                if q >= 2:
                    act.wait_ge(y_ready, GPQ * (q - 1))
                act.dma_start(yS[:, q % 2, :], xT[:, q * QC:(q + 1) * QC]).then_inc(xT_in, 16)
                act.wait_ge(xT_in, 16 * (q + 1))
                if q == 0:
                    act.wait_ge(oma_ready, 1)
                act.activation(yS[:, q % 2, :], yS[:, q % 2, :], ACT.Copy, scale=oma[:, 0:1]).then_inc(xTs_scaled, 1)

            def prep_tangent(G):
                act.wait_ge(u_ready, G + 1)
                act.activation(lnu, uu, ACT.Ln).then_inc(ln_ready, 1)
                act.wait_ge(fac_ready, G + 1)
                act.wait_ge(xTp_ready, G)
                act.wait_ge(xt_out, G * 16)
                for k in range(GT):
                    ins = act.activation(xt_st[:, k * D:(k + 1) * D], x1b[:, k * D:(k + 1) * D], ACT.Copy,
                                         scale=fac[:, k:k + 1])
                ins.then_inc(xt_ready, 1)
                act.wait_ge(xt_ready, G + 1)
                act.dma_start(xt_d[G], xt_st).then_inc(xt_out, 16)

            def prep_rows(G):
                act.wait_ge(xTp_ready, G + 1)
                act.wait_ge(proj_ready, G)
                act.activation(xTt, ps_e(G)[:, 2 * BANK:2 * BANK + GC], ACT.Copy).then_inc(xTt_ready, 1)
                act.wait_ge(proj_ready, G + 1)
                act.wait_ge(rows_out, G * 16)
                act.activation(rows, ps_e(G)[0:2, 3 * BANK:3 * BANK + GC], ACT.Copy).then_inc(rows_ready, 1)
                act.wait_ge(rows_ready, G + 1)
                act.dma_start(plcl_d[:, ds(G * GC, GC)], rows).then_inc(rows_out, 16)

            def trip(q, t, prev):
                G = (q - 1) * GPQ + t
                act.wait_ge(var_ready, G)
                act.dma_start(xn, x_g[G]).then_inc(xn_in, 16)
                if prev:
                    prep_tangent(G - 1)
                act.wait_ge(var_ready, G + 1)
                act.activation(std, mv[:, :, 1], ACT.Sqrt, bias=epsc[:, 0:1]).then_inc(std_ready, 1)
                act.wait_ge(x1_ready, G + 1)
                act.dma_start(x1_d[G], x1b).then_inc(x1_out, 16)
                for k in range(GT):
                    ins = act.activation(junk[:, k * D:(k + 1) * D], x1b[:, k * D:(k + 1) * D], ACT.Square,
                                         accum_out=ss[:, k:k + 1])
                ins.then_inc(ss_ready, 1)
                act.wait_ge(ss_ready, G + 1)
                act.activation(nrm, ss, ACT.Sqrt).then_inc(nrm_ready, 1)
                if prev:
                    prep_rows(G - 1)

            def ps_e(G):
                return ps[ep_set[0]]

            ep_set = [0]
            act.wait_ge(ident_ready, 4)
            load_xT(0)
            for q in range(1, NQ + 1):
                ep_set[0] = (q - 1) % 2
                if q < NQ:
                    load_xT(q)
                for t in range(peeled(q)):
                    trip(q, t, prev=(q, t) != (1, 0))
                with act.Fori(peeled(q), GPQ) as t:
                    trip(q, t, prev=True)
            prep_tangent(NG - 1)
            prep_rows(NG - 1)

            act.wait_ge(rows_out, 16 * NG)
            act.wait_ge(xt_out, 16 * NG)
            act.wait_ge(x1_out, 16 * NG)
            act.wait_ge(proj_ready, NG)
            act.wait_ge(prcr_ready, NG)
            act.preload_act_table(ACT.Sigmoid)
            with act.Fori(0, NPAN) as it:
                for ph in range(PHASES):
                    _, _, dist, to_j, _ = PH[ph]
                    cols = lJ if to_j else lI[:, ds(it % 2, 1)].rearrange("p a r c -> p (a r) c")
                    tile0 = it * TPP if to_j or dist == 0 else ((it + dist) % NPAN) * TPP
                    if to_j:
                        act.wait_ge(lJ_in, (it * 3 + dist) * 32)
                    elif ph == 0:
                        act.wait_ge(lI_in, (it + 1) * 32)
                    for u in range(UNITS):
                        n = ph * UNITS + u
                        free = act.lower_val(it * UPI + n + 1)
                        constant_wait(act)
                        act.wait_ge(psig_free, free)
                        act.activation(psig[:, n % PSIG, :], cols[:, 0, :], ACT.Sigmoid,
                                       bias=prcr[:, ds((tile0 + u) * 2, 1)]).then_inc(p_ready, 1)
                        constant_wait(act)
                        act.wait_ge(csig_free, free)
                        act.activation(csig[:, n % CSIG, :], cols[:, 1, :], ACT.Sigmoid,
                                       bias=prcr[:, ds((tile0 + u) * 2 + 1, 1)]).then_inc(c_ready, 1)

            act.wait_ge(csig_free, NPAN * UPI + CSIG)
            for g in range(N // BANK):
                act.wait_ge(u_copied, g + 1)
                for k in range(BANK // D):
                    tile = g * (BANK // D) + k
                    ins = act.activation(res_o[:, tile * D:(tile + 1) * D],
                                         uN[:, tile * D:(tile + 1) * D],
                                         ACT.Square, accum_out=fs[:, 0, tile:tile + 1])
                ins.then_inc(u_sumsq, 1)
            act.wait_ge(u_sumsq, N // BANK)
            act.activation(fs[:, 1, :], fs[:, 0, :], ACT.Sqrt).then_inc(f_act, 1)
            act.wait_ge(f_step, 1)
            act.activation(fs[:, 3, :], fs[:, 2, :], ACT.Tanh).then_inc(f_act, 1)
            act.wait_ge(fvar_ready, NPAN)
            act.activation(fs[:, 9, :], mvf[:, :, 1], ACT.Sqrt, bias=epsc[:, 0:1]).then_inc(f_act, 1)

        @block.vector
        def _(dve):
            steps = [0]

            def step(base, ins):
                steps[0] += 1
                ins.then_inc(dve_step, 1)
                dve.wait_ge(dve_step, base + steps[0])

            dve.wait_ge(const_in, 16 * N_CONST)
            dve.tensor_scalar(oma[:, :], alph[:, :], -1.0, 1.0, ALU.mult, ALU.add).then_inc(oma_ready, 1)
            dve.wait_ge(oma_ready, 1)

            def add_slot(q, t, s):
                m = (q * TRIPS + t) * SLOTS + s
                dve.wait_ge(g_in[s], (q * TRIPS + t + 1) * 32)
                for tt in range(2):
                    dst = accS[:, q % 2, :].rearrange("p (b c) -> p b c", b=BPQ)
                    dve.tensor_tensor(out=dst, in0=dst, in1=g0[s][:, :, tt, :], op=ALU.add).then_inc(acc_step, 1)
                    dve.wait_ge(acc_step, m * 2 + tt + 1)

            def degrees_and_y(q, t, base):
                E = ps[(q - 1) % 2]
                G = (q - 1) * GPQ + t
                dve.wait_ge(deg_ready, G + 1)
                step(base, dve.tensor_scalar(dg, E[:, 0:GC], alph[:, 0:1], oma[:, 0:1], ALU.mult, ALU.add))
                step(base, dve.scalar_tensor_tensor(out=sf, in0=dg, scalar=0.0, in1=dg, op0=ALU.is_equal, op1=ALU.add))
                step(base, dve.reciprocal(rc, sf))
                step(base, dve.scalar_tensor_tensor(out=sf, in0=dg, scalar=0.0, in1=rc, op0=ALU.not_equal, op1=ALU.mult))
                dve.tensor_tensor(out=y_st, in0=yS[:, (q - 1) % 2, ds(t * GC, GC)], in1=sf, op=ALU.mult) \
                    .then_inc(y_ready, 1)

            def log_map_argument(G, base):
                dve.wait_ge(nrm_ready, G + 1)
                step(base, dve.tensor_scalar(nrm2, nrm, MIN_NORM, None, ALU.max))
                step(base, dve.tensor_scalar(clp, nrm2, CLIP, None, ALU.min))
                step(base, dve.tensor_scalar(om, clp, -1.0, 1.0, ALU.mult, ALU.add))
                step(base, dve.reciprocal(rom, om))
                step(base, dve.scalar_tensor_tensor(out=tt2, in0=clp, scalar=2.0, in1=rom, op0=ALU.mult, op1=ALU.mult))
                dve.tensor_scalar(uu, tt2, 1.0, None, ALU.add).then_inc(u_ready, 1)

            def log_map_factor(G, base):
                dve.wait_ge(ln_ready, G + 1)
                step(base, dve.tensor_scalar(um1, uu, -1.0, None, ALU.add))
                step(base, dve.tensor_scalar(zz, um1, 0.0, None, ALU.is_equal))
                step(base, dve.tensor_tensor(out=ums, in0=um1, in1=zz, op=ALU.add))
                step(base, dve.reciprocal(um1, ums))
                step(base, dve.tensor_tensor(out=ums, in0=lnu, in1=um1, op=ALU.mult))
                step(base, dve.tensor_tensor(out=ums, in0=ums, in1=zz, op=ALU.add))
                step(base, dve.scalar_tensor_tensor(out=l1p, in0=ums, scalar=0.5, in1=tt2, op0=ALU.mult, op1=ALU.mult))
                step(base, dve.reciprocal(um1, nrm2))
                dve.tensor_tensor(out=fac, in0=l1p, in1=um1, op=ALU.mult).then_inc(fac_ready, 1)

            def residual_stats(q, t, base):
                E = ps[(q - 1) % 2]
                G = (q - 1) * GPQ + t
                dve.wait_ge(h_ready, G + 1)
                dve.wait_ge(xn_in, (G + 1) * 16)
                step(base, dve.scalar_tensor_tensor(out=r_st, in0=E[:, BANK:BANK + GC], scalar=0.0, in1=xn,
                                                    op0=ALU.max, op1=ALU.add))
                for k in range(GT):
                    ins = dve.bn_stats(bst[:, k, :], r_st[:, k * D:(k + 1) * D])
                steps[0] += 1
                ins.then_inc(dve_step, 1)
                stats = dve.lower_val(base + steps[0])
                constant_wait(dve)
                dve.wait_ge(dve_step, stats)
                for k in range(GT):
                    ins = dve.bn_aggr(mv[:, k, :], bst[:, k, :])
                ins.then_inc(var_ready, 1)

            def normalise(G, base):
                dve.wait_ge(std_ready, G + 1)
                step(base, dve.reciprocal(rstd, std))
                dve.wait_ge(x1_out, G * 16)
                for k in range(GT):
                    ins = dve.tensor_scalar(x1b[:, k * D:(k + 1) * D], r_st[:, k * D:(k + 1) * D],
                                            mv[:, k, 0:1], rstd[:, k:k + 1], ALU.subtract, ALU.mult)
                ins.then_inc(x1_ready, 1)

            def row_biases(q, G):
                E = ps[(q - 1) % 2]
                dve.wait_ge(proj_ready, G + 1)
                dve.tensor_tensor(out=prcr[:, ds(G * GT * 2, GT * 2)],
                                  in0=E[:, GC:GC + 2 * GT], in1=bpc2[:, :], op=ALU.add) \
                    .then_inc(prcr_ready, 1)

            def trip(q, t, prev, base):
                main = q < NQ
                epi = q > 0
                G = (q - 1) * GPQ + t
                if epi:
                    degrees_and_y(q, t, base)
                if prev:
                    log_map_argument(G - 1, base)
                if main:
                    add_slot(q, t, 0)
                if epi:
                    residual_stats(q, t, base)
                if prev:
                    log_map_factor(G - 1, base)
                if main:
                    add_slot(q, t, 1)
                if prev:
                    dve.wait_ge(xt_ready, G)
                if epi:
                    normalise(G, base)
                if main:
                    add_slot(q, t, 2)
                if prev:
                    row_biases(q, G - 1)
                if main:
                    add_slot(q, t, 3)

            for k in range(GT):
                dve.tensor_copy(bpc2[:, 2 * k:2 * k + 2], bpc[:, :]).then_inc(bpc2_ready, 1)
            dve.wait_ge(bpc2_ready, GT)
            for q in range(NQ + 1):
                if q < NQ:
                    dve.wait_ge(acc_zeroed, q + 1)
                if q > 0:
                    dve.wait_ge(pe_slots, q * TRIPS * SLOTS)
                    dve.wait_ge(xTs_scaled, q)
                    yq = yS[:, (q - 1) % 2, :]
                    dve.scalar_tensor_tensor(out=yq, in0=ps[(q - 1) % 2][:, :], scalar=alph[:, 0:1], in1=yq,
                                             op0=ALU.mult, op1=ALU.add).then_inc(y_evac, 1)
                    dve.wait_ge(y_evac, q)
                for t in range(peeled(q)):
                    trip(q, t, prev=q > 0 and (q, t) != (1, 0), base=0)
                before = steps[0]
                with dve.Fori(peeled(q), TRIPS) as t:
                    count = STEPS_PER_TRIP if q > 0 else 0
                    trip(q, t, prev=q > 0, base=(t - peeled(q)) * count)
                assert steps[0] - before == count
                steps[0] = before + (TRIPS - peeled(q)) * count
            log_map_argument(NG - 1, 0)
            log_map_factor(NG - 1, 0)
            row_biases(NQ, NG - 1)

            def evacuate(it, n_evac, ph, panel):
                dve.wait_ge(psig_free, it * UPI + (ph + 1) * UNITS + PSIG)
                dve.wait_ge(evac_done, it * EVACS + n_evac + 1)
                dst = acc[:, ds(panel * BP, BP)]
                dve.tensor_tensor(out=dst, in0=OUTP[PH[ph][OUT]], in1=dst, op=ALU.add).then_inc(evac_done, 1)

            dve.wait_ge(sup_zeroed, 1)
            with dve.Fori(0, NPAN) as it:
                for ph in range(PHASES):
                    for u in range(UNITS):
                        n = ph * UNITS + u
                        T = TP[n % TBUF]
                        dve.wait_ge(t_ready, it * UPI + n + 1)
                        dve.wait_ge(c_ready, it * UPI + n + 1)
                        dve.tensor_tensor(out=T, in0=T, in1=csig[:, n % CSIG, :], op=ALU.mult).then_inc(csig_free, 1)
                        dve.wait_ge(csig_free, it * UPI + n + 1 + CSIG)
                        dve.wait_ge(nat_ready, it * UPI + n + 1)
                        dve.tensor_tensor(out=psig[:, n % PSIG, :], in0=T, in1=psig[:, n % PSIG, :], op=ALU.add) \
                            .then_inc(kt_ready, 1)
                        if u == 1 and ph % 2 == 1:
                            d = PH[ph - 1][DIST]
                            evacuate(it, (ph - 1) // 2, ph - 1, (it + d) % NPAN)
                evacuate(it, EVACS - 1, PHASES - 1, it)

            dve.wait_ge(t_ready, NPAN * UPI)
            dve.wait_ge(nat_ready, NPAN * UPI)
            for g in range(N // BANK):
                dve.wait_ge(uT_ready, g + 1)
                dve.tensor_copy(uN[:, g * BANK:(g + 1) * BANK], ps[0][:, (g % 4) * BANK:(g % 4 + 1) * BANK]) \
                    .then_inc(u_copied, 1)
            s_ss, s_n, s_nm, s_th, s_rn, s_s1, s_n2, s_r2, s_s, s_sd, s_rs = [fs[:, k, :] for k in range(11)]
            dve.wait_ge(f_act, 1)
            dve.tensor_scalar(s_nm, s_n, MIN_NORM, None, ALU.max).then_inc(f_step, 1)
            dve.wait_ge(f_step, 1)
            step(0, dve.reciprocal(s_rn, s_nm))
            dve.wait_ge(f_act, 2)
            step(0, dve.tensor_tensor(out=s_s1, in0=s_th, in1=s_rn, op=ALU.mult))
            step(0, dve.tensor_tensor(out=s_n2, in0=s_s1, in1=s_n, op=ALU.mult))
            step(0, dve.tensor_scalar(s_n2, s_n2, MIN_NORM, None, ALU.max))
            step(0, dve.reciprocal(s_r2, s_n2))
            step(0, dve.tensor_scalar(s_r2, s_r2, MAXNORM, 1.0, ALU.mult, ALU.min))
            step(0, dve.tensor_tensor(out=s_s, in0=s_s1, in1=s_r2, op=ALU.mult))
            dve.wait_ge(u_copied, N // BANK)
            for p in range(NPAN):
                if p % 2 == 0:
                    dve.wait_ge(x1f_in[p // 2], 16)
                tiles = range(p * TPP, (p + 1) * TPP)
                for k in tiles:
                    ins = dve.scalar_tensor_tensor(out=uN[:, k * D:(k + 1) * D], in0=uN[:, k * D:(k + 1) * D],
                                                   scalar=s_s[:, k:k + 1], in1=x1f[:, k * D:(k + 1) * D],
                                                   op0=ALU.mult, op1=ALU.add)
                step(0, ins)
                for k in tiles:
                    ins = dve.bn_stats(bstf[:, k, :], uN[:, k * D:(k + 1) * D])
                step(0, ins)
                for k in tiles:
                    ins = dve.bn_aggr(mvf[:, k, :], bstf[:, k, :])
                ins.then_inc(fvar_ready, 1)
            dve.wait_ge(f_act, 3)
            dve.wait_ge(fvar_ready, NPAN)
            step(0, dve.reciprocal(s_rs, s_sd))
            for p in range(NPAN):
                for k in range(p * TPP, (p + 1) * TPP):
                    ins = dve.tensor_scalar(res_o[:, k * D:(k + 1) * D], uN[:, k * D:(k + 1) * D],
                                            mvf[:, k, 0:1], s_rs[:, k:k + 1], ALU.subtract, ALU.mult)
                ins.then_inc(o_ready, 1)

        @block.tensor
        def _(pe):
            pe.wait_ge(const_in, 16 * N_CONST)
            pe.wait_ge(ident_ready, 4)

            def main_slot(q, t, s, first, last):
                n = q * TRIPS + t
                if s % 2 == 0:
                    pe.wait_ge(xg_in[s // 2], (n + 1) * 16)
                pe.wait_ge(g_in[s], (n + 1) * 32)
                for tt in range(2):
                    lhs = xg[:, s // 2, ((s % 2) * 2 + tt) * D:((s % 2) * 2 + tt + 1) * D]
                    for b in range(BPQ):
                        for h in range(BP // BANK):
                            k = b * (BP // BANK) + h
                            ins = pe.matmul(ps[q % 2][:, k * BANK:(k + 1) * BANK], lhs,
                                            g0[s][:, b, tt, h * BANK:(h + 1) * BANK],
                                            start=(first and s == 0 and tt == 0),
                                            stop=(last and s == SLOTS - 1 and tt == 1))
                ins.then_inc(pe_slots, 1)

            def degree_sums(q, t, first):
                G = (q - 1) * GPQ + t
                if not first:
                    pe.wait_ge(prcr_ready, G - 1)
                pe.wait_ge(y_ready, G)
                pe.matmul(ps[(q - 1) % 2][:, 0:GC], ones[:, :], accS[:, (q - 1) % 2, ds(t * GC, GC)],
                          start=True, stop=True).then_inc(deg_ready, 1)

            def linear(q, t):
                E = ps[(q - 1) % 2]
                G = (q - 1) * GPQ + t
                pe.wait_ge(y_ready, G + 1)
                pe.wait_ge(var_ready, G)
                for k in range(GT):
                    o = E[:, BANK + k * D:BANK + (k + 1) * D]
                    pe.matmul(o, y_st[:, k * P:(k + 1) * P], WTs[:, :], start=True, stop=False)
                    ins = pe.matmul(o, ones[0:1, :], brow[:, :], start=False, stop=True)
                ins.then_inc(h_ready, 1)

            def turn_tangent(q, G):
                E = ps[(q - 1) % 2]
                pe.wait_ge(xt_ready, G + 1)
                pe.wait_ge(xTt_ready, G)
                for k in range(GT):
                    ins = pe.transpose(E[:, 2 * BANK + k * P:2 * BANK + (k + 1) * P], xt_st[:, k * D:(k + 1) * D],
                                       ident[:, :])
                ins.then_inc(xTp_ready, 1)

            def projections(q, G):
                E = ps[(q - 1) % 2]
                pe.wait_ge(xTt_ready, G + 1)
                pe.wait_ge(rows_ready, G)
                pe.wait_ge(prcr_ready, G)
                pe.matmul(E[0:2, 3 * BANK:3 * BANK + GC], wl[:, :], xTt, start=True, stop=True)
                for k in range(GT):
                    ins = pe.matmul(E[:, GC + 2 * k:GC + 2 * k + 2], xTt[:, k * P:(k + 1) * P],
                                    wr[:, :], start=True, stop=True)
                ins.then_inc(proj_ready, 1)

            def trip(q, t, prev, first=False, last=False):
                main = q < NQ
                epi = q > 0
                G = (q - 1) * GPQ + t
                if epi:
                    degree_sums(q, t, first=q == 1 and first)
                if main:
                    main_slot(q, t, 0, first, last)
                if epi:
                    linear(q, t)
                if main:
                    main_slot(q, t, 1, first, last)
                if prev:
                    turn_tangent(q, G - 1)
                if main:
                    main_slot(q, t, 2, first, last)
                if prev:
                    projections(q, G - 1)
                if main:
                    main_slot(q, t, 3, first, last)

            for q in range(NQ + 1):
                if q > 0:
                    pe.wait_ge(y_evac, q)
                    pe.wait_ge(acc_step, q * TRIPS * SLOTS * 2)
                if 2 <= q < NQ:
                    pe.wait_ge(y_ready, (q - 1) * GPQ)
                    pe.wait_ge(var_ready, (q - 1) * GPQ)
                    pe.wait_ge(rows_ready, (q - 1) * GPQ - 1)
                    pe.wait_ge(prcr_ready, (q - 1) * GPQ - 1)
                for t in range(peeled(q)):
                    trip(q, t, prev=q > 0 and (q, t) != (1, 0), first=t == 0)
                with pe.Fori(peeled(q), TRIPS - 1) as t:
                    trip(q, t, prev=q > 0)
                trip(q, TRIPS - 1, prev=q > 0, last=True)
            turn_tangent(NQ, NG - 1)
            projections(NQ, NG - 1)

            def transposes(it, ph, u):
                n = ph * UNITS + u
                blk = PH[ph][TRN]
                if u == 0:
                    for c in range(CHUNKS):
                        pe.wait_ge(c_in[(blk % 3) * CHUNKS + c], (it * 3 + blk // 3 + 1) * 16)
                pe.wait_ge(kt_ready, it * UPI + n + 1)
                for v in range(TPP):
                    at = ((blk % 3) * CHUNKS + v // 2) * CH + (v % 2) * BP + u * P
                    ins = pe.transpose(TP[n % TBUF][:, v * P:(v + 1) * P], ring[:, at:at + P], ident[:, :])
                ins.then_inc(t_ready, 1)

            def products(it, ph, u):
                n = ph * UNITS + u
                _, _, dist, to_j, o = PH[ph]
                from_i = to_j or dist == 0
                if u == 0:
                    if from_i:
                        pe.wait_ge(xtI_in, (it + 1) * 16)
                    else:
                        pe.wait_ge(xtJ_in, (it * 4 + dist) * 16)
                    pe.wait_ge(evac_done, it * EVACS + ph // 2 + 1)
                pe.wait_ge(kt_ready, it * UPI + n + 1 + TBUF)
                xt = xtI if from_i else xtJ
                for h in range(BP // BANK):
                    ins = pe.matmul(OUTP[o][:, h * BANK:(h + 1) * BANK], xt[:, u * D:(u + 1) * D],
                                    psig[:, n % PSIG, h * BANK:(h + 1) * BANK],
                                    start=(u == 0 and (o == 1 or ph == 1)),
                                    stop=(u == UNITS - 1 and (o == 1 or ph == PHASES - 1)))
                ins.then_inc(psig_free, 1)

            pe.wait_ge(rows_ready, NG)
            pe.wait_ge(prcr_ready, NG)
            with pe.Fori(0, NPAN) as it:
                transposes(it, 0, 0)
                for n in range(UPI):
                    if n + 1 < UPI:
                        transposes(it, (n + 1) // UNITS, (n + 1) % UNITS)
                    products(it, n // UNITS, n % UNITS)

            pe.wait_ge(evac_done, NPAN * EVACS + 1)
            for g in range(N // BANK):
                if g >= 4:
                    pe.wait_ge(u_copied, g - 3)
                for k in range(BANK // D):
                    tile = g * (BANK // D) + k
                    ins = pe.transpose(ps[0][:, (g % 4) * BANK + k * D:(g % 4) * BANK + (k + 1) * D],
                                       acc[:, tile * P:(tile + 1) * P], ident[:, :])
                ins.then_inc(uT_ready, 1)


def kernel(x, adj, L0_gnn_t, L0_gnn_alpha, L0_gnn_W, L0_gnn_b, L1_gnn_w_par, L1_gnn_b_par, L1_gnn_w_chi, L1_gnn_b_chi):
    import numpy as np
    import concourse.bacc as bacc
    from concourse.bass_utils import run_bass_kernel_spmd

    x, adj = np.asarray(x), np.asarray(adj)
    arrays = {
        "x_g": x.reshape(NG, GT, P, D).transpose(0, 2, 1, 3).reshape(NG, P, GC),
        "xT": x.T,
        "g_blk": adj.T.reshape(NPAN, BP, NPAN, BP).transpose(0, 2, 1, 3),
        "WT": np.asarray(L0_gnn_W).T,
        "b_row": np.asarray(L0_gnn_b),
        "alpha": np.asarray(L0_gnn_alpha),
        "w_par": np.asarray(L1_gnn_w_par), "b_par": np.asarray(L1_gnn_b_par),
        "w_chi": np.asarray(L1_gnn_w_chi), "b_chi": np.asarray(L1_gnn_b_chi),
    }
    arrays = {f"in_{k}": np.ascontiguousarray(v) for k, v in arrays.items()}
    nc = bacc.Bacc("TRN2", target_bir_lowering=False, num_devices=1)
    args = [nc.dram_tensor(k, v.shape, mybir.dt.from_np(v.dtype), kind="ExternalInput").ap() for k, v in arrays.items()]
    out = nc.dram_tensor("out_0", (N, D), F32, kind="ExternalOutput").ap()
    adj_resnorm_kernel(nc, *args, out)
    r = run_bass_kernel_spmd(nc, [arrays], core_ids=[0])
    return r.results[0]["out_0"]
```

```python
from contextlib import ExitStack

import concourse.bass as bass
from concourse import mybir


F32 = mybir.dt.float32
ALU = mybir.AluOpType
ACT = mybir.ActivationFunctionType
ds = bass.ds

N = 8192
P = 128
D = 128
BP = 1024
NPAN = N // BP
TPP = BP // P
BANK = 512

NQ = 4
QC = N // NQ
BPQ = QC // BP
SLOTS = 4
STEPS = 2 * SLOTS
TRIPS = N // (2 * P * STEPS)
GC = 512
GT = GC // P
GPQ = QC // GC
NG = N // GC

CHUNKS = 4
CH = 2 * BP
UNITS = TPP
PHASES = 8
UPI = UNITS * PHASES
PSIG, CSIG, TBUF = 4, 2, 2
STEPS_PER_TRIP = 20
LN_EPS = 1e-5
MIN_NORM = 1e-15
CLIP = 1.0 - 1e-7
MAXNORM = 1.0 - 1e-5

NAT, TRN, DIST, TO_J, OUT = range(5)
X1, Y1, X2, Y2, X4, Y4, DG, X3, Y3 = range(9)
PH = [
    (Y1, X1, 1, False, 0), (X1, Y1, 1, True, 1),
    (Y2, X2, 2, False, 0), (X2, Y2, 2, True, 1),
    (Y4, X4, 4, False, 0), (DG, DG, 0, False, 0),
    (Y3, X3, 3, False, 0), (X3, Y3, 3, True, 1),
]
BLOCK_DIST = {X1: 1, Y1: 1, X2: 2, Y2: 2, X4: 4, Y4: 4, DG: 0, X3: 3, Y3: 3}
XTJ_PHASES = [0, 2, 4, 6]
LJ_PHASES = [1, 3, 7]
LAG = 2
EVAC = [(7, 0), (1, 2), (3, 4), (6, 7)]
EVACS = len(EVAC)
OUT_A_FIRST, OUT_A_LAST = 0, 6
NBLK = 9


def adj_resnorm_kernel(nc, x_g, xT, g_blk, WT, b_row, alpha, w_par, b_par, w_chi, b_chi, out):
    with ExitStack() as ctx:
        def sb(name, shape):
            return ctx.enter_context(nc.sbuf_tensor(name, shape, F32))

        def sem(name):
            return ctx.enter_context(nc.semaphore(name))

        ring = sb("ring", [P, 3 * CHUNKS * CH])
        acc = sb("acc", [P, N])
        psig = sb("psig", [P, 4, BP])
        csig = sb("csig", [P, 2, BP])
        lI = sb("lI", [P, 2, 2, BP])
        lJ = sb("lJ", [P, 2, BP])
        xtI = sb("xtI", [P, TPP * D])
        xtJ = sb("xtJ", [P, TPP * D])
        prcr = sb("prcr", [P, N // P * 2])
        ones = sb("ones", [P, P])
        ident = sb("ident", [P, P])
        WTs = sb("WTs", [P, D])
        wl = sb("wl", [P, 2])
        wr = sb("wr", [P, 2])
        bpc = sb("bpc", [P, 2])
        bpc2 = sb("bpc2", [P, 2 * GT])
        brow = sb("brow", [1, D])
        alph = sb("alph", [P, 1])
        oma = sb("oma", [P, 1])
        epsc = sb("epsc", [P, 1])
        mv = sb("mv", [P, GT, 2])
        bst = sb("bst", [P, GT, 6])
        small = sb("small", [P, 16, GT])
        (std, rstd, ss, nrm, nrm2, clp, om, rom, tt2, uu, lnu, fac, um1, zz, ums, l1p) = [small[:, k, :] for k in range(16)]
        fs = sb("fs", [P, 11, N // P])
        mvf = sb("mvf", [P, N // P, 2])
        bstf = sb("bstf", [P, N // P, 6])

        accS = acc[:, 0:2 * QC].rearrange("p (q c) -> p q c", q=2)
        xg = acc[:, 2 * QC:2 * QC + 2 * BANK].rearrange("p (h c) -> p h c", h=2)
        yS = lI[:, :, :, :].rearrange("p a b c -> p a (b c)")
        y_st, r_st, x1b, xt_st, xn, xTt = [psig[:, k // 2, (k % 2) * GC:(k % 2 + 1) * GC] for k in range(6)]
        rows = psig[0:2, 3, 0:GC]
        dg, sf, rc, junk = [csig[:, k // 2, (k % 2) * GC:(k % 2 + 1) * GC] for k in range(4)]
        g0 = [ring[:, s * 2 * CH:(s + 1) * 2 * CH].rearrange("p (b t c) -> p b t c", b=BPQ, t=2) for s in range(SLOTS)]

        uN = ring[:, 0:N]
        x1f = ring[:, N:2 * N]
        res_o = ring[:, 2 * N:3 * N]

        ps = [ctx.enter_context(nc.psum_tensor(f"ps{k}", [P, QC], F32)) for k in range(2)]
        TP = [ps[0][:, 0:BP], ps[0][:, BP:2 * BP]]
        OUTP = [ps[1][:, 0:BP], ps[1][:, BP:2 * BP]]

        x1_d = nc.dram_tensor("x1_d", [NG, P, GC], F32)
        xt_d = nc.dram_tensor("xt_d", [NG, P, GC], F32)
        plcl_d = nc.dram_tensor("plcl_d", [2, N], F32)

        const_in = sem("const_in")
        ident_ready = sem("ident_ready")
        oma_ready = sem("oma_ready")
        bpc2_ready = sem("bpc2_ready")
        g_in = [sem(f"g_in{s}") for s in range(SLOTS)]
        xg_in = [sem(f"xg_in{h}") for h in range(2)]
        pe_slots = sem("pe_slots")
        acc_step = sem("acc_step")
        acc_zeroed = sem("acc_zeroed")
        xT_in = sem("xT_in")
        xTs_scaled = sem("xTs_scaled")
        y_evac = sem("y_evac")
        deg_ready = sem("deg_ready")
        dve_step = sem("dve_step")
        y_ready = sem("y_ready")
        h_ready = sem("h_ready")
        xn_in = sem("xn_in")
        var_ready = sem("var_ready")
        std_ready = sem("std_ready")
        x1_ready = sem("x1_ready")
        x1_out = sem("x1_out")
        ss_ready = sem("ss_ready")
        nrm_ready = sem("nrm_ready")
        u_ready = sem("u_ready")
        ln_ready = sem("ln_ready")
        fac_ready = sem("fac_ready")
        xt_ready = sem("xt_ready")
        xt_out = sem("xt_out")
        xTp_ready = sem("xTp_ready")
        xTt_ready = sem("xTt_ready")
        proj_ready = sem("proj_ready")
        rows_ready = sem("rows_ready")
        rows_out = sem("rows_out")
        prcr_ready = sem("prcr_ready")

        c_in = [sem(f"c_in{k}") for k in range(3 * CHUNKS)]
        lI_in = sem("lI_in")
        lJ_in = sem("lJ_in")
        xtI_in = sem("xtI_in")
        xtJ_in = sem("xtJ_in")
        p_ready = sem("p_ready")
        c_ready = sem("c_ready")
        t_ready = sem("t_ready")
        nat_ready = sem("nat_ready")
        psig_free = sem("psig_free")
        csig_free = sem("csig_free")
        kt_ready = sem("kt_ready")
        sup_zeroed = sem("sup_zeroed")
        psig_zeroed = sem("psig_zeroed")
        evac_done = sem("evac_done")

        x1f_in = [sem(f"x1f_in{h}") for h in range(4)]
        uT_ready = sem("uT_ready")
        u_copied = sem("u_copied")
        u_sumsq = sem("u_sumsq")
        f_step = sem("f_step")
        f_act = sem("f_act")
        fvar_ready = sem("fvar_ready")
        o_ready = sem("o_ready")
        out_done = sem("out_done")

        N_CONST = 9

        def constant_wait(eng):
            eng.wait_ge(const_in, 16 * N_CONST)

        def peeled(q):
            return 2 if q == 1 else 1

        block = ctx.enter_context(nc.Block())

        @block.sync
        def _(sp):
            for dst, src in (
                (WTs[:, :], WT), (brow[:, :], b_row.rearrange("(a d) -> a d", a=1)),
                (alph[:, :], alpha.rearrange("(a d) -> a d", a=1).to_broadcast([P, 1])),
                (bpc[:, 0:1], b_par.rearrange("(a d) -> a d", a=1).to_broadcast([P, 1])),
                (bpc[:, 1:2], b_chi.rearrange("(a d) -> a d", a=1).to_broadcast([P, 1])),
                (wl[:, 0:1], w_par[0:D].rearrange("(d a) -> d a", a=1)),
                (wl[:, 1:2], w_chi[0:D].rearrange("(d a) -> d a", a=1)),
                (wr[:, 0:1], w_par[D:2 * D].rearrange("(d a) -> d a", a=1)),
                (wr[:, 1:2], w_chi[D:2 * D].rearrange("(d a) -> d a", a=1)),
            ):
                sp.dma_start(dst, src).then_inc(const_in, 16)

            def load_trip(q, t, first=False):
                n = q * TRIPS + t
                for s in range(STEPS):
                    slot, xh = s % SLOTS, (s // 2) % 2
                    fresh = first and s < SLOTS
                    if s % 2 == 0:
                        if not fresh:
                            used = sp.lower_val(n * STEPS + s - 2)
                            constant_wait(sp)
                            sp.wait_ge(pe_slots, used)
                        sp.dma_start(xg[:, xh, :], x_g[t * (STEPS // 2) + s // 2]).then_inc(xg_in[xh], 16)
                    if not fresh:
                        used = sp.lower_val(n * STEPS + s - 3)
                        added = sp.lower_val((n * STEPS + s - 3) * 2)
                        constant_wait(sp)
                        sp.wait_ge(pe_slots, used)
                        sp.wait_ge(acc_step, added)
                    for b in range(BPQ):
                        sp.dma_start(g0[slot][:, b], g_blk[t * 2 + s // SLOTS, q * BPQ + b,
                                                           slot * 2 * P:(slot + 1) * 2 * P, :]
                                     .rearrange("(t p) c -> p t c", p=P)).then_inc(g_in[slot], 16)

            for q in range(NQ):
                if q == 0:
                    load_trip(0, 0, first=True)
                with sp.Fori(1 if q == 0 else 0, TRIPS) as t:
                    load_trip(q, t)

            def users(blk):
                return [([k for k in range(PHASES) if PH[k][use] == blk] or [None])[0] for use in (TRN, NAT)]

            def load_block(it, b, prev_it=None):
                other = (it + BLOCK_DIST[b]) % NPAN
                src = g_blk[it, other] if b in (X1, X2, X3, X4) else g_blk[other, it]
                for c in range(CHUNKS):
                    if prev_it is not None:
                        trn, nat = users((b - 3) % NBLK)
                        turned = None if trn is None else sp.lower_val(prev_it * UPI + (trn + 1) * UNITS)
                        used = None if nat is None else sp.lower_val(prev_it * UPI + nat * UNITS + 2 * c + 2)
                        constant_wait(sp)
                        if trn is not None:
                            sp.wait_ge(t_ready, turned)
                        if nat is not None:
                            sp.wait_ge(nat_ready, used)
                    k = (b % 3) * CHUNKS + c
                    sp.dma_start(ring[:, k * CH:(k + 1) * CH].rearrange("p (t c) -> p t c", t=2),
                                 src[c * 2 * P:(c + 1) * 2 * P, :].rearrange("(t p) c -> p t c", p=P)) \
                        .then_inc(c_in[k], 16)

            def load_xt(dst, panel, done):
                sp.dma_start(dst[:, :].rearrange("p (g c) -> p g c", g=BP // GC),
                             xt_d[ds(panel * (BP // GC), BP // GC)].rearrange("g p c -> p g c")).then_inc(done, 16)

            def load_l(dst, panel, done):
                for r in range(2):
                    sp.dma_start(dst[:, r, :], plcl_d[r:r + 1, ds(panel * BP, BP)].to_broadcast([P, BP])) \
                        .then_inc(done, 16)

            def phase_end(it, ph):
                return sp.lower_val(it * UPI + (ph + 1) * UNITS + PSIG)

            sp.wait_ge(pe_slots, NQ * TRIPS * STEPS)
            sp.wait_ge(acc_step, NQ * TRIPS * STEPS * 2)
            for b in (X1, Y1, X2):
                load_block(0, b)
            sp.wait_ge(xt_out, 16 * NG)
            sp.wait_ge(rows_out, 16 * NG)
            sp.wait_ge(y_ready, NG)
            load_l(lI[:, 0], 0, lI_in)
            load_xt(xtI, 0, xtI_in)
            load_xt(xtJ, 1, xtJ_in)
            load_l(lJ, 1, lJ_in)

            def next_xtJ(it, ph, panel):
                used = phase_end(it, ph)
                constant_wait(sp)
                sp.wait_ge(psig_free, used)
                load_xt(xtJ, panel % NPAN, xtJ_in)

            def next_lJ(it, ph, panel):
                used = sp.lower_val(it * UPI + (ph + 1) * UNITS)
                constant_wait(sp)
                sp.wait_ge(c_ready, used)
                sp.wait_ge(p_ready, used)
                load_l(lJ, panel % NPAN, lJ_in)

            def iteration(it, last):
                next_xtJ(it, 0, it + 2)
                load_block(it, Y2, it)
                next_lJ(it, 1, it + 2)
                load_block(it, X4, it)
                next_xtJ(it, 2, it + 4)
                load_block(it, Y4, it)
                next_lJ(it, 3, it + 3)
                load_block(it, DG, it)
                load_block(it, Y3, it)
                next_xtJ(it, 4, it + 3)
                load_block(it, X3, it)
                if last:
                    return
                load_l(lI[:, (it + 1) % 2], it + 1, lI_in)
                load_block(it + 1, X1, it)
                next_xtJ(it, 6, it + 2)
                load_block(it + 1, Y1, it)
                next_lJ(it, 7, it + 2)
                load_block(it + 1, X2, it)
                used = phase_end(it, 7)
                constant_wait(sp)
                sp.wait_ge(psig_free, used)
                load_xt(xtI, it + 1, xtI_in)

            with sp.Fori(0, NPAN - 1) as it:
                iteration(it, False)
            iteration(NPAN - 1, True)

            sp.wait_ge(x1_out, 16 * NG)
            sp.wait_ge(t_ready, NPAN * UPI)
            sp.wait_ge(nat_ready, NPAN * UPI)
            for h in range(4):
                g = NG // 4
                sp.dma_start(x1f[:, h * g * GC:(h + 1) * g * GC].rearrange("p (g c) -> p g c", g=g),
                             x1_d[h * g:(h + 1) * g].rearrange("g p c -> p g c")).then_inc(x1f_in[h], 16)
            for p in range(NPAN):
                sp.wait_ge(o_ready, p + 1)
                sp.dma_start(out[p * BP:(p + 1) * BP, :].rearrange("(t p) d -> p t d", p=P),
                             res_o[:, p * BP:(p + 1) * BP].rearrange("p (t d) -> p t d", t=TPP)).then_inc(out_done, 16)
            sp.wait_ge(out_done, 16 * NPAN)

        @block.gpsimd
        def _(pool):
            pool.memset(ones[:, :], 1.0).then_inc(ident_ready, 1)
            pool.memset(epsc[:, :], LN_EPS).then_inc(ident_ready, 1)
            pool.memset(ident[:, :], 0.0).then_inc(ident_ready, 1)
            pool.wait_ge(ident_ready, 3)
            pool.affine_select(out=ident[:, :], in_=ident[:, :], compare_op=ALU.not_equal, fill=1.0, base=0,
                               pattern=[[-1, P]], channel_multiplier=1).then_inc(ident_ready, 1)
            pool.sem_inc(psig_free, PSIG - LAG)
            pool.sem_inc(csig_free, CSIG)
            pool.sem_inc(kt_ready, TBUF)
            pool.sem_inc(evac_done, 1)

            for q in range(NQ):
                if q >= 2:
                    pool.wait_ge(deg_ready, GPQ * (q - 1))
                pool.memset(accS[:, q % 2, :], 0.0).then_inc(acc_zeroed, 1)

            pool.wait_ge(deg_ready, NG)
            pool.wait_ge(pe_slots, NQ * TRIPS * STEPS)
            pool.memset(acc[:, :], 0.0).then_inc(sup_zeroed, 1)
            pool.wait_ge(rows_out, 16 * NG)
            pool.wait_ge(xt_out, 16 * NG)
            pool.wait_ge(x1_out, 16 * NG)
            pool.wait_ge(proj_ready, NG)
            pool.wait_ge(prcr_ready, NG)
            pool.memset(psig[:, PSIG - LAG:PSIG, :], 0.0).then_inc(psig_zeroed, 1)

            with pool.Fori(0, NPAN) as it:
                for ph in range(PHASES):
                    blk = PH[ph][NAT]
                    for u in range(UNITS):
                        n = ph * UNITS + u
                        k = (blk % 3) * CHUNKS + u // 2
                        if u % 2 == 0:
                            pool.wait_ge(c_in[k], (it * 3 + blk // 3 + 1) * 16)
                        pool.wait_ge(p_ready, it * UPI + n + 1)
                        pool.tensor_tensor(out=psig[:, n % PSIG, :], in0=psig[:, n % PSIG, :],
                                           in1=ring[:, k * CH + (u % 2) * BP:k * CH + (u % 2 + 1) * BP],
                                           op=ALU.mult).then_inc(nat_ready, 1)

        @block.scalar
        def _(act):
            def load_xT(q):
                if q >= 2:
                    act.wait_ge(y_ready, GPQ * (q - 1))
                act.dma_start(yS[:, q % 2, :], xT[:, q * QC:(q + 1) * QC]).then_inc(xT_in, 16)
                act.wait_ge(xT_in, 16 * (q + 1))
                if q == 0:
                    act.wait_ge(oma_ready, 1)
                act.activation(yS[:, q % 2, :], yS[:, q % 2, :], ACT.Copy, scale=oma[:, 0:1]).then_inc(xTs_scaled, 1)

            def prep_tangent(G):
                act.wait_ge(u_ready, G + 1)
                act.activation(lnu, uu, ACT.Ln).then_inc(ln_ready, 1)
                act.wait_ge(fac_ready, G + 1)
                act.wait_ge(xTp_ready, G)
                act.wait_ge(xt_out, G * 16)
                for k in range(GT):
                    ins = act.activation(xt_st[:, k * D:(k + 1) * D], x1b[:, k * D:(k + 1) * D], ACT.Copy,
                                         scale=fac[:, k:k + 1])
                ins.then_inc(xt_ready, 1)
                act.wait_ge(xt_ready, G + 1)
                act.dma_start(xt_d[G], xt_st).then_inc(xt_out, 16)

            def prep_rows(G):
                act.wait_ge(xTp_ready, G + 1)
                act.wait_ge(proj_ready, G)
                act.activation(xTt, ps_e(G)[:, 2 * BANK:2 * BANK + GC], ACT.Copy).then_inc(xTt_ready, 1)
                act.wait_ge(proj_ready, G + 1)
                act.wait_ge(rows_out, G * 16)
                act.activation(rows, ps_e(G)[0:2, 3 * BANK:3 * BANK + GC], ACT.Copy).then_inc(rows_ready, 1)
                act.wait_ge(rows_ready, G + 1)
                act.dma_start(plcl_d[:, ds(G * GC, GC)], rows).then_inc(rows_out, 16)

            def trip(q, t, prev):
                G = (q - 1) * GPQ + t
                act.wait_ge(var_ready, G)
                act.dma_start(xn, x_g[G]).then_inc(xn_in, 16)
                if prev:
                    prep_tangent(G - 1)
                act.wait_ge(var_ready, G + 1)
                act.activation(std, mv[:, :, 1], ACT.Sqrt, bias=epsc[:, 0:1]).then_inc(std_ready, 1)
                act.wait_ge(x1_ready, G + 1)
                act.dma_start(x1_d[G], x1b).then_inc(x1_out, 16)
                for k in range(GT):
                    ins = act.activation(junk[:, k * D:(k + 1) * D], x1b[:, k * D:(k + 1) * D], ACT.Square,
                                         accum_out=ss[:, k:k + 1])
                ins.then_inc(ss_ready, 1)
                act.wait_ge(ss_ready, G + 1)
                act.activation(nrm, ss, ACT.Sqrt).then_inc(nrm_ready, 1)
                if prev:
                    prep_rows(G - 1)

            def ps_e(G):
                return ps[ep_set[0]]

            ep_set = [0]
            act.wait_ge(ident_ready, 4)
            load_xT(0)
            for q in range(1, NQ + 1):
                ep_set[0] = (q - 1) % 2
                if q < NQ:
                    load_xT(q)
                for t in range(peeled(q)):
                    trip(q, t, prev=(q, t) != (1, 0))
                with act.Fori(peeled(q), GPQ) as t:
                    trip(q, t, prev=True)
            prep_tangent(NG - 1)
            prep_rows(NG - 1)

            act.wait_ge(rows_out, 16 * NG)
            act.wait_ge(xt_out, 16 * NG)
            act.wait_ge(x1_out, 16 * NG)
            act.wait_ge(proj_ready, NG)
            act.wait_ge(prcr_ready, NG)
            act.preload_act_table(ACT.Sigmoid)
            with act.Fori(0, NPAN) as it:
                for ph in range(PHASES):
                    _, _, dist, to_j, _ = PH[ph]
                    cols = lJ if to_j else lI[:, ds(it % 2, 1)].rearrange("p a r c -> p (a r) c")
                    tile0 = it * TPP if to_j or dist == 0 else ((it + dist) % NPAN) * TPP
                    if to_j:
                        act.wait_ge(lJ_in, (it * len(LJ_PHASES) + LJ_PHASES.index(ph) + 1) * 32)
                    elif ph == 0:
                        act.wait_ge(lI_in, (it + 1) * 32)
                    for u in range(UNITS):
                        n = ph * UNITS + u
                        free = act.lower_val(it * UPI + n + 1)
                        constant_wait(act)
                        act.wait_ge(psig_free, free)
                        act.activation(psig[:, n % PSIG, :], cols[:, 0, :], ACT.Sigmoid,
                                       bias=prcr[:, ds((tile0 + u) * 2, 1)]).then_inc(p_ready, 1)
                        constant_wait(act)
                        act.wait_ge(csig_free, free)
                        act.activation(csig[:, n % CSIG, :], cols[:, 1, :], ACT.Sigmoid,
                                       bias=prcr[:, ds((tile0 + u) * 2 + 1, 1)]).then_inc(c_ready, 1)

            act.wait_ge(csig_free, NPAN * UPI + CSIG)
            for g in range(N // BANK):
                act.wait_ge(u_copied, g + 1)
                for k in range(BANK // D):
                    tile = g * (BANK // D) + k
                    ins = act.activation(res_o[:, tile * D:(tile + 1) * D],
                                         uN[:, tile * D:(tile + 1) * D],
                                         ACT.Square, accum_out=fs[:, 0, tile:tile + 1])
                ins.then_inc(u_sumsq, 1)
            act.wait_ge(u_sumsq, N // BANK)
            act.activation(fs[:, 1, :], fs[:, 0, :], ACT.Sqrt).then_inc(f_act, 1)
            act.wait_ge(f_step, 1)
            act.activation(fs[:, 3, :], fs[:, 2, :], ACT.Tanh).then_inc(f_act, 1)
            act.wait_ge(fvar_ready, NPAN)
            act.activation(fs[:, 9, :], mvf[:, :, 1], ACT.Sqrt, bias=epsc[:, 0:1]).then_inc(f_act, 1)

        @block.vector
        def _(dve):
            steps = [0]

            def step(base, ins):
                steps[0] += 1
                ins.then_inc(dve_step, 1)
                dve.wait_ge(dve_step, base + steps[0])

            dve.wait_ge(const_in, 16 * N_CONST)
            dve.tensor_scalar(oma[:, :], alph[:, :], -1.0, 1.0, ALU.mult, ALU.add).then_inc(oma_ready, 1)
            dve.wait_ge(oma_ready, 1)

            def add_slot(q, t, s):
                m = (q * TRIPS + t) * STEPS + s
                dve.wait_ge(g_in[s % SLOTS], ((q * TRIPS + t) * 2 + s // SLOTS + 1) * 32)
                for tt in range(2):
                    dst = accS[:, q % 2, :].rearrange("p (b c) -> p b c", b=BPQ)
                    dve.tensor_tensor(out=dst, in0=dst, in1=g0[s % SLOTS][:, :, tt, :], op=ALU.add).then_inc(acc_step, 1)
                    dve.wait_ge(acc_step, m * 2 + tt + 1)

            def degrees_and_y(q, t, base):
                E = ps[(q - 1) % 2]
                G = (q - 1) * GPQ + t
                dve.wait_ge(deg_ready, G + 1)
                step(base, dve.tensor_scalar(dg, E[:, 0:GC], alph[:, 0:1], oma[:, 0:1], ALU.mult, ALU.add))
                step(base, dve.scalar_tensor_tensor(out=sf, in0=dg, scalar=0.0, in1=dg, op0=ALU.is_equal, op1=ALU.add))
                step(base, dve.reciprocal(rc, sf))
                step(base, dve.scalar_tensor_tensor(out=sf, in0=dg, scalar=0.0, in1=rc, op0=ALU.not_equal, op1=ALU.mult))
                dve.tensor_tensor(out=y_st, in0=yS[:, (q - 1) % 2, ds(t * GC, GC)], in1=sf, op=ALU.mult) \
                    .then_inc(y_ready, 1)

            def log_map_argument(G, base):
                dve.wait_ge(nrm_ready, G + 1)
                step(base, dve.tensor_scalar(nrm2, nrm, MIN_NORM, None, ALU.max))
                step(base, dve.tensor_scalar(clp, nrm2, CLIP, None, ALU.min))
                step(base, dve.tensor_scalar(om, clp, -1.0, 1.0, ALU.mult, ALU.add))
                step(base, dve.reciprocal(rom, om))
                step(base, dve.scalar_tensor_tensor(out=tt2, in0=clp, scalar=2.0, in1=rom, op0=ALU.mult, op1=ALU.mult))
                dve.tensor_scalar(uu, tt2, 1.0, None, ALU.add).then_inc(u_ready, 1)

            def log_map_factor(G, base):
                dve.wait_ge(ln_ready, G + 1)
                step(base, dve.tensor_scalar(um1, uu, -1.0, None, ALU.add))
                step(base, dve.tensor_scalar(zz, um1, 0.0, None, ALU.is_equal))
                step(base, dve.tensor_tensor(out=ums, in0=um1, in1=zz, op=ALU.add))
                step(base, dve.reciprocal(um1, ums))
                step(base, dve.tensor_tensor(out=ums, in0=lnu, in1=um1, op=ALU.mult))
                step(base, dve.tensor_tensor(out=ums, in0=ums, in1=zz, op=ALU.add))
                step(base, dve.scalar_tensor_tensor(out=l1p, in0=ums, scalar=0.5, in1=tt2, op0=ALU.mult, op1=ALU.mult))
                step(base, dve.reciprocal(um1, nrm2))
                dve.tensor_tensor(out=fac, in0=l1p, in1=um1, op=ALU.mult).then_inc(fac_ready, 1)

            def residual_stats(q, t, base):
                E = ps[(q - 1) % 2]
                G = (q - 1) * GPQ + t
                dve.wait_ge(h_ready, G + 1)
                dve.wait_ge(xn_in, (G + 1) * 16)
                step(base, dve.scalar_tensor_tensor(out=r_st, in0=E[:, BANK:BANK + GC], scalar=0.0, in1=xn,
                                                    op0=ALU.max, op1=ALU.add))
                for k in range(GT):
                    ins = dve.bn_stats(bst[:, k, :], r_st[:, k * D:(k + 1) * D])
                steps[0] += 1
                ins.then_inc(dve_step, 1)
                stats = dve.lower_val(base + steps[0])
                constant_wait(dve)
                dve.wait_ge(dve_step, stats)
                for k in range(GT):
                    ins = dve.bn_aggr(mv[:, k, :], bst[:, k, :])
                ins.then_inc(var_ready, 1)

            def normalise(G, base):
                dve.wait_ge(std_ready, G + 1)
                step(base, dve.reciprocal(rstd, std))
                dve.wait_ge(x1_out, G * 16)
                for k in range(GT):
                    ins = dve.tensor_scalar(x1b[:, k * D:(k + 1) * D], r_st[:, k * D:(k + 1) * D],
                                            mv[:, k, 0:1], rstd[:, k:k + 1], ALU.subtract, ALU.mult)
                ins.then_inc(x1_ready, 1)

            def row_biases(q, G):
                E = ps[(q - 1) % 2]
                dve.wait_ge(proj_ready, G + 1)
                dve.tensor_tensor(out=prcr[:, ds(G * GT * 2, GT * 2)],
                                  in0=E[:, 2 * BANK:2 * BANK + 2 * GT], in1=bpc2[:, :], op=ALU.add) \
                    .then_inc(prcr_ready, 1)

            def trip(q, t, prev, base):
                main = q < NQ
                epi = q > 0
                G = (q - 1) * GPQ + t
                if epi:
                    degrees_and_y(q, t, base)
                if prev:
                    log_map_argument(G - 1, base)
                if main:
                    add_slot(q, t, 0)
                    add_slot(q, t, 1)
                if epi:
                    residual_stats(q, t, base)
                if prev:
                    log_map_factor(G - 1, base)
                if main:
                    add_slot(q, t, 2)
                    add_slot(q, t, 3)
                if prev:
                    dve.wait_ge(xt_ready, G)
                if epi:
                    normalise(G, base)
                if main:
                    add_slot(q, t, 4)
                    add_slot(q, t, 5)
                if prev:
                    row_biases(q, G - 1)
                if main:
                    add_slot(q, t, 6)
                    add_slot(q, t, 7)

            for k in range(GT):
                dve.tensor_copy(bpc2[:, 2 * k:2 * k + 2], bpc[:, :]).then_inc(bpc2_ready, 1)
            dve.wait_ge(bpc2_ready, GT)
            for q in range(NQ + 1):
                if q < NQ:
                    dve.wait_ge(acc_zeroed, q + 1)
                if q > 0:
                    dve.wait_ge(pe_slots, q * TRIPS * STEPS)
                    dve.wait_ge(xTs_scaled, q)
                    yq = yS[:, (q - 1) % 2, :]
                    dve.scalar_tensor_tensor(out=yq, in0=ps[(q - 1) % 2][:, :], scalar=alph[:, 0:1], in1=yq,
                                             op0=ALU.mult, op1=ALU.add).then_inc(y_evac, 1)
                    dve.wait_ge(y_evac, q)
                for t in range(peeled(q)):
                    trip(q, t, prev=q > 0 and (q, t) != (1, 0), base=0)
                before = steps[0]
                with dve.Fori(peeled(q), TRIPS) as t:
                    count = STEPS_PER_TRIP if q > 0 else 0
                    trip(q, t, prev=q > 0, base=(t - peeled(q)) * count)
                assert steps[0] - before == count
                steps[0] = before + (TRIPS - peeled(q)) * count
            log_map_argument(NG - 1, 0)
            log_map_factor(NG - 1, 0)
            row_biases(NQ, NG - 1)

            def evacuate(products_done, evacs_before, ph, panel):
                dve.wait_ge(psig_free, products_done + PSIG)
                dve.wait_ge(evac_done, evacs_before + 1)
                dst = acc[:, ds(panel * BP, BP)]
                dve.tensor_tensor(out=dst, in0=OUTP[PH[ph][OUT]], in1=dst, op=ALU.add).then_inc(evac_done, 1)

            dve.wait_ge(sup_zeroed, 1)
            with dve.Fori(0, NPAN) as it:
                for ph in range(PHASES):
                    for u in range(UNITS):
                        n = ph * UNITS + u
                        T = TP[n % TBUF]
                        dve.wait_ge(t_ready, it * UPI + n + 1)
                        dve.wait_ge(c_ready, it * UPI + n + 1)
                        dve.tensor_tensor(out=T, in0=T, in1=csig[:, n % CSIG, :], op=ALU.mult).then_inc(csig_free, 1)
                        dve.wait_ge(csig_free, it * UPI + n + 1 + CSIG)
                        dve.wait_ge(nat_ready, it * UPI + n + 1)
                        dve.tensor_tensor(out=psig[:, n % PSIG, :], in0=T, in1=psig[:, n % PSIG, :], op=ALU.add) \
                            .then_inc(kt_ready, 1)
                        for e, (of, during) in enumerate(EVAC):
                            if (ph, u) == (during, LAG + 1):
                                if of == 7:
                                    evacuate(it * UPI, it * EVACS + e, of, (it + 2) % NPAN)
                                else:
                                    to = (it + PH[of][DIST]) % NPAN if PH[of][TO_J] else it
                                    evacuate(it * UPI + (of + 1) * UNITS, it * EVACS + e, of, to)
            evacuate(NPAN * UPI, NPAN * EVACS, 7, (NPAN + 2) % NPAN)

            dve.wait_ge(t_ready, NPAN * UPI)
            dve.wait_ge(nat_ready, NPAN * UPI)
            for g in range(N // BANK):
                dve.wait_ge(uT_ready, g + 1)
                dve.tensor_copy(uN[:, g * BANK:(g + 1) * BANK], ps[0][:, (g % 4) * BANK:(g % 4 + 1) * BANK]) \
                    .then_inc(u_copied, 1)
            s_ss, s_n, s_nm, s_th, s_rn, s_s1, s_n2, s_r2, s_s, s_sd, s_rs = [fs[:, k, :] for k in range(11)]
            dve.wait_ge(f_act, 1)
            dve.tensor_scalar(s_nm, s_n, MIN_NORM, None, ALU.max).then_inc(f_step, 1)
            dve.wait_ge(f_step, 1)
            step(0, dve.reciprocal(s_rn, s_nm))
            dve.wait_ge(f_act, 2)
            step(0, dve.tensor_tensor(out=s_s1, in0=s_th, in1=s_rn, op=ALU.mult))
            step(0, dve.tensor_tensor(out=s_n2, in0=s_s1, in1=s_n, op=ALU.mult))
            step(0, dve.tensor_scalar(s_n2, s_n2, MIN_NORM, None, ALU.max))
            step(0, dve.reciprocal(s_r2, s_n2))
            step(0, dve.tensor_scalar(s_r2, s_r2, MAXNORM, 1.0, ALU.mult, ALU.min))
            step(0, dve.tensor_tensor(out=s_s, in0=s_s1, in1=s_r2, op=ALU.mult))
            dve.wait_ge(u_copied, N // BANK)
            for p in range(NPAN):
                if p % 2 == 0:
                    dve.wait_ge(x1f_in[p // 2], 16)
                tiles = range(p * TPP, (p + 1) * TPP)
                for k in tiles:
                    ins = dve.scalar_tensor_tensor(out=uN[:, k * D:(k + 1) * D], in0=uN[:, k * D:(k + 1) * D],
                                                   scalar=s_s[:, k:k + 1], in1=x1f[:, k * D:(k + 1) * D],
                                                   op0=ALU.mult, op1=ALU.add)
                step(0, ins)
                for k in tiles:
                    ins = dve.bn_stats(bstf[:, k, :], uN[:, k * D:(k + 1) * D])
                step(0, ins)
                for k in tiles:
                    ins = dve.bn_aggr(mvf[:, k, :], bstf[:, k, :])
                ins.then_inc(fvar_ready, 1)
            dve.wait_ge(f_act, 3)
            dve.wait_ge(fvar_ready, NPAN)
            step(0, dve.reciprocal(s_rs, s_sd))
            for p in range(NPAN):
                for k in range(p * TPP, (p + 1) * TPP):
                    ins = dve.tensor_scalar(res_o[:, k * D:(k + 1) * D], uN[:, k * D:(k + 1) * D],
                                            mvf[:, k, 0:1], s_rs[:, k:k + 1], ALU.subtract, ALU.mult)
                ins.then_inc(o_ready, 1)

        @block.tensor
        def _(pe):
            pe.wait_ge(const_in, 16 * N_CONST)
            pe.wait_ge(ident_ready, 4)

            def main_step(q, t, s, first, last):
                n = (q * TRIPS + t) * 2 + s // SLOTS
                slot, xh = s % SLOTS, (s // 2) % 2
                if s % 2 == 0:
                    pe.wait_ge(xg_in[xh], (n + 1) * 16)
                pe.wait_ge(g_in[slot], (n + 1) * 32)
                for tt in range(2):
                    lhs = xg[:, xh, ((s % 2) * 2 + tt) * D:((s % 2) * 2 + tt + 1) * D]
                    for b in range(BPQ):
                        for h in range(BP // BANK):
                            k = b * (BP // BANK) + h
                            ins = pe.matmul(ps[q % 2][:, k * BANK:(k + 1) * BANK], lhs,
                                            g0[slot][:, b, tt, h * BANK:(h + 1) * BANK],
                                            start=(first and s == 0 and tt == 0),
                                            stop=(last and s == STEPS - 1 and tt == 1))
                ins.then_inc(pe_slots, 1)

            def degree_sums(q, t):
                G = (q - 1) * GPQ + t
                pe.wait_ge(y_ready, G)
                pe.matmul(ps[(q - 1) % 2][:, 0:GC], ones[:, :], accS[:, (q - 1) % 2, ds(t * GC, GC)],
                          start=True, stop=True).then_inc(deg_ready, 1)

            def linear(q, t):
                E = ps[(q - 1) % 2]
                G = (q - 1) * GPQ + t
                pe.wait_ge(y_ready, G + 1)
                pe.wait_ge(var_ready, G)
                for k in range(GT):
                    o = E[:, BANK + k * D:BANK + (k + 1) * D]
                    pe.matmul(o, y_st[:, k * P:(k + 1) * P], WTs[:, :], start=True, stop=False)
                    ins = pe.matmul(o, ones[0:1, :], brow[:, :], start=False, stop=True)
                ins.then_inc(h_ready, 1)

            def turn_tangent(q, G):
                E = ps[(q - 1) % 2]
                pe.wait_ge(xt_ready, G + 1)
                pe.wait_ge(xTt_ready, G)
                pe.wait_ge(prcr_ready, G)
                for k in range(GT):
                    ins = pe.transpose(E[:, 2 * BANK + k * P:2 * BANK + (k + 1) * P], xt_st[:, k * D:(k + 1) * D],
                                       ident[:, :])
                ins.then_inc(xTp_ready, 1)

            def projections(q, G):
                E = ps[(q - 1) % 2]
                pe.wait_ge(xTt_ready, G + 1)
                pe.wait_ge(rows_ready, G)
                pe.matmul(E[0:2, 3 * BANK:3 * BANK + GC], wl[:, :], xTt, start=True, stop=True)
                for k in range(GT):
                    ins = pe.matmul(E[:, 2 * BANK + 2 * k:2 * BANK + 2 * k + 2], xTt[:, k * P:(k + 1) * P],
                                    wr[:, :], start=True, stop=True)
                ins.then_inc(proj_ready, 1)

            def trip(q, t, prev, first=False, last=False):
                main = q < NQ
                epi = q > 0
                G = (q - 1) * GPQ + t
                if epi:
                    degree_sums(q, t)
                if main:
                    main_step(q, t, 0, first, last)
                    main_step(q, t, 1, first, last)
                if epi:
                    linear(q, t)
                if main:
                    main_step(q, t, 2, first, last)
                    main_step(q, t, 3, first, last)
                if prev:
                    turn_tangent(q, G - 1)
                if main:
                    main_step(q, t, 4, first, last)
                    main_step(q, t, 5, first, last)
                if prev:
                    projections(q, G - 1)
                if main:
                    main_step(q, t, 6, first, last)
                    main_step(q, t, 7, first, last)

            for q in range(NQ + 1):
                if q > 0:
                    pe.wait_ge(y_evac, q)
                    pe.wait_ge(acc_step, q * TRIPS * STEPS * 2)
                if 2 <= q < NQ:
                    pe.wait_ge(y_ready, (q - 1) * GPQ)
                    pe.wait_ge(var_ready, (q - 1) * GPQ)
                    pe.wait_ge(rows_ready, (q - 1) * GPQ - 1)
                    pe.wait_ge(prcr_ready, (q - 1) * GPQ - 1)
                for t in range(peeled(q)):
                    trip(q, t, prev=q > 0 and (q, t) != (1, 0), first=t == 0)
                with pe.Fori(peeled(q), TRIPS - 1) as t:
                    trip(q, t, prev=q > 0)
                trip(q, TRIPS - 1, prev=q > 0, last=True)
            turn_tangent(NQ, NG - 1)
            projections(NQ, NG - 1)

            def transposes(it, ph, u):
                n = ph * UNITS + u
                blk = PH[ph][TRN]
                if u == 0:
                    for c in range(CHUNKS):
                        pe.wait_ge(c_in[(blk % 3) * CHUNKS + c], (it * 3 + blk // 3 + 1) * 16)
                pe.wait_ge(kt_ready, it * UPI + n + 1)
                for v in range(TPP):
                    at = ((blk % 3) * CHUNKS + v // 2) * CH + (v % 2) * BP + u * P
                    ins = pe.transpose(TP[n % TBUF][:, v * P:(v + 1) * P], ring[:, at:at + P], ident[:, :])
                ins.then_inc(t_ready, 1)

            def products(it, n):
                ph, u = divmod(n % UPI, UNITS)
                _, _, dist, to_j, o = PH[ph]
                from_i = to_j or dist == 0
                if u == 0:
                    if from_i:
                        pe.wait_ge(xtI_in, (it + 1) * 16)
                    else:
                        pe.wait_ge(xtJ_in, (it * len(XTJ_PHASES) + XTJ_PHASES.index(ph) + 1) * 16)
                    if o == 1 or ph == OUT_A_FIRST:
                        pe.wait_ge(evac_done, it * EVACS + sum(during < ph for _, during in EVAC) + 1)
                pe.wait_ge(kt_ready, it * UPI + n + 1 + TBUF)
                xt = xtI if from_i else xtJ
                for h in range(BP // BANK):
                    ins = pe.matmul(OUTP[o][:, h * BANK:(h + 1) * BANK], xt[:, u * D:(u + 1) * D],
                                    psig[:, n % PSIG, h * BANK:(h + 1) * BANK],
                                    start=(u == 0 and (o == 1 or ph == OUT_A_FIRST)),
                                    stop=(u == UNITS - 1 and (o == 1 or ph == OUT_A_LAST)))
                ins.then_inc(psig_free, 1)

            pe.wait_ge(rows_ready, NG)
            pe.wait_ge(prcr_ready, NG)
            pe.wait_ge(psig_zeroed, 1)
            zeros = psig[:, PSIG - LAG, :]
            for h in range(BP // BANK):
                pe.matmul(OUTP[1][:, h * BANK:(h + 1) * BANK], zeros[:, 0:P], zeros[:, 0:BANK], start=True, stop=False)
            pe.wait_ge(xtI_in, 16)
            with pe.Fori(0, NPAN) as it:
                for n in range(UPI):
                    transposes(it, n // UNITS, n % UNITS)
                    products(it, n - LAG)
            for n in range(UPI - LAG, UPI):
                products(NPAN - 1, n)

            pe.wait_ge(evac_done, NPAN * EVACS + 2)
            for g in range(N // BANK):
                if g >= 4:
                    pe.wait_ge(u_copied, g - 3)
                for k in range(BANK // D):
                    tile = g * (BANK // D) + k
                    ins = pe.transpose(ps[0][:, (g % 4) * BANK + k * D:(g % 4) * BANK + (k + 1) * D],
                                       acc[:, tile * P:(tile + 1) * P], ident[:, :])
                ins.then_inc(uT_ready, 1)


def kernel(x, adj, L0_gnn_t, L0_gnn_alpha, L0_gnn_W, L0_gnn_b, L1_gnn_w_par, L1_gnn_b_par, L1_gnn_w_chi, L1_gnn_b_chi):
    import numpy as np
    import concourse.bacc as bacc
    from concourse.bass_utils import run_bass_kernel_spmd

    x, adj = np.asarray(x), np.asarray(adj)
    arrays = {
        "x_g": x.reshape(NG, GT, P, D).transpose(0, 2, 1, 3).reshape(NG, P, GC),
        "xT": x.T,
        "g_blk": adj.T.reshape(NPAN, BP, NPAN, BP).transpose(0, 2, 1, 3),
        "WT": np.asarray(L0_gnn_W).T,
        "b_row": np.asarray(L0_gnn_b),
        "alpha": np.asarray(L0_gnn_alpha),
        "w_par": np.asarray(L1_gnn_w_par), "b_par": np.asarray(L1_gnn_b_par),
        "w_chi": np.asarray(L1_gnn_w_chi), "b_chi": np.asarray(L1_gnn_b_chi),
    }
    arrays = {f"in_{k}": np.ascontiguousarray(v) for k, v in arrays.items()}
    nc = bacc.Bacc("TRN2", target_bir_lowering=False, num_devices=1)
    args = [nc.dram_tensor(k, v.shape, mybir.dt.from_np(v.dtype), kind="ExternalInput").ap() for k, v in arrays.items()]
    out = nc.dram_tensor("out_0", (N, D), F32, kind="ExternalOutput").ap()
    adj_resnorm_kernel(nc, *args, out)
    r = run_bass_kernel_spmd(nc, [arrays], core_ids=[0])
    return r.results[0]["out_0"]
```

```python
from contextlib import ExitStack

import concourse.bass as bass
from concourse import mybir


F32 = mybir.dt.float32
ALU = mybir.AluOpType
ACT = mybir.ActivationFunctionType
ds = bass.ds

N = 8192
P = 128
D = 128
BP = 1024
NPAN = N // BP
TPP = BP // P
BANK = 512

NQ = 4
QC = N // NQ
BPQ = QC // BP
SLOTS = 4
STEPS = 2 * SLOTS
TRIPS = N // (2 * P * STEPS)
GC = 512
GT = GC // P
GPQ = QC // GC
NG = N // GC

CHUNKS = 4
CH = 2 * BP
CHUNK_ROWS = 2 * P
UNITS = TPP
PHASES = 8
UPI = UNITS * PHASES
PSIG, CSIG, TBUF = 4, 4, 2
STEPS_PER_TRIP = 21
LN_EPS = 1e-5
MIN_NORM = 1e-15
CLIP = 1.0 - 1e-7
MAXNORM = 1.0 - 1e-5

NAT, TRN, DIST, TO_J, OUT = range(5)
Y1, X1, DG, X2, Y2, Y4, X4, Y3, X3 = range(9)
NBLK = 9
PH = [
    (X1, Y1, 1, True, 1), (Y1, X1, 1, False, 0),
    (DG, DG, 0, False, 0),
    (Y2, X2, 2, False, 0), (X2, Y2, 2, True, 1),
    (Y4, X4, 4, False, 0),
    (X3, Y3, 3, True, 1), (Y3, X3, 3, False, 0),
]
BLOCK_DIST = {X1: 1, Y1: 1, X2: 2, Y2: 2, X4: 4, Y4: 4, DG: 0, X3: 3, Y3: 3}
XTJ_PHASES = [1, 3, 5, 7]
LJ_PHASES = [0, 4, 6]
LI_FIRST, LI_LAST = 1, 7
XTI_LAST = 6
TURNED = 768
DIRC = BP - TURNED
TURNED_CHUNKS = -(-TURNED // CHUNK_ROWS)
DIR_SLOTS = 4
DIR_LOADS = UPI // 2 // DIR_SLOTS
AHEAD = 4
DIR_CREDIT = 2 * DIR_SLOTS - AHEAD - 1
LAG = 2
EVAC = [(7, 0), (0, 1), (4, 5), (6, 7)]
EVACS = len(EVAC)
OUT_A_FIRST, OUT_A_LAST = 1, 7

LAST = NPAN - 1
NORM_BY_PE = [((LAST + d) % NPAN, 1) for d in (4, 5, 6, 7)]
NORM_BY_ACT = [((LAST + d) % NPAN, d + 1) for d in (1, 2, 3)] + [(LAST, 5)]
ORDER = NORM_BY_ACT + NORM_BY_PE
PE_TILES = slice(NORM_BY_PE[0][0] * TPP, (NORM_BY_PE[-1][0] + 1) * TPP)
GPP = BP // BANK
BY_POOL = 4


def phase_of(blk, use):
    return next((ph for ph in range(PHASES) if PH[ph][use] == blk), None)


def turned_chunk(c):
    return c * CHUNK_ROWS < TURNED


def holders(s, c):
    return [b for b in range(s, NBLK, 3) if phase_of(b, NAT) is not None or turned_chunk(c)]


def arrivals(it, b, c):
    h = holders(b % 3, c)
    return it * len(h) + h.index(b) + 1


def adj_resnorm_kernel(nc, x_g, xT, g_blk, a_cols, WT, b_row, alpha, w_par, b_par, w_chi, b_chi, out):
    with ExitStack() as ctx:
        def sb(name, shape):
            return ctx.enter_context(nc.sbuf_tensor(name, shape, F32))

        def sem(name):
            return ctx.enter_context(nc.semaphore(name))

        ring = sb("ring", [P, 3 * CHUNKS * CH])
        acc = sb("acc", [P, N])
        psig = sb("psig", [P, PSIG, BP])
        csig = sb("csig", [P, CSIG, BP])
        adir = sb("adir", [P, DIR_SLOTS, 2, DIRC])
        scores = sb("scores", [P, 2, 2, BP])
        lI, lJ = scores[:, 0], scores[:, 1]
        xtI = sb("xtI", [P, TPP * D])
        xtJ = sb("xtJ", [P, TPP * D])
        prcr = sb("prcr", [P, N // P * 2])
        ones = sb("ones", [P, P])
        ident = sb("ident", [P, P])
        WTs = sb("WTs", [P, D])
        wl = sb("wl", [P, 2])
        wr = sb("wr", [P, 2])
        bpc = sb("bpc", [P, 2])
        bpc2 = sb("bpc2", [P, 2 * GT])
        bb = sb("bb", [P, D])
        alph = sb("alph", [P, 1])
        oma = sb("oma", [P, 1])
        epsc = sb("epsc", [P, 1])
        mv = sb("mv", [P, GT, 2])
        bst = sb("bst", [P, GT, 6])
        small = sb("small", [P, 20, GT])
        (std, rstd, ss, nrm, nrm2, clp, om, rom, tt2, uu, lnu, fac, um1, zz, ums, l1p,
         dg, sf, rc, inv) = [small[:, k, :] for k in range(20)]
        fs = sb("fs", [P, 11, N // P])
        mvf = sb("mvf", [P, N // P, 2])
        bstf = sb("bstf", [P, N // P, 6])

        accS = acc[:, 0:2 * QC].rearrange("p (q c) -> p q c", q=2)
        xg = acc[:, 2 * QC:2 * QC + 2 * BANK].rearrange("p (h c) -> p h c", h=2)
        yS = scores[:, :, :, :].rearrange("p a b c -> p a (b c)")
        y_st, r_st, x1b, xt_st, xn, xTt, s_st, rows = [psig[:, k // 2, (k % 2) * GC:(k % 2 + 1) * GC] for k in range(8)]
        rows = rows[0:2, :]
        junk = csig[:, 0, 0:GC]
        g0 = [ring[:, s * 2 * CH:(s + 1) * 2 * CH].rearrange("p (b t c) -> p b t c", b=BPQ, t=2) for s in range(SLOTS)]

        x1f = ring[:, 0:N]
        uN = ring[:, N:2 * N]
        res_o = ring[:, 2 * N:3 * N]

        squares = [scores[:, k // 2, k % 2, :] for k in range(4)]

        s_n, s_nm, s_th, s_rn, s_s1, s_n2, s_s, s_sd, s_rs, s_mb, s_ss = [fs[:, k, :] for k in range(11)]

        def group_of_u(g):
            at = ORDER[g // GPP][0] * BP + g % GPP * BANK
            return uN[:, at:at + BANK]

        ps = [ctx.enter_context(nc.psum_tensor(f"ps{k}", [P, QC], F32)) for k in range(2)]
        TP = [ps[0][:, 0:BP], ps[0][:, BP:2 * BP]]
        OUTP = [ps[1][:, 0:BP], ps[1][:, BP:2 * BP]]
        sumsq = OUTP[1][:, 0:N // P]

        x1_d = nc.dram_tensor("x1_d", [NG, P, GC], F32)
        xt_d = nc.dram_tensor("xt_d", [NG, P, GC], F32)
        plcl_d = nc.dram_tensor("plcl_d", [2, N], F32)

        const_in = sem("const_in")
        ident_ready = sem("ident_ready")
        oma_ready = sem("oma_ready")
        bpc2_ready = sem("bpc2_ready")
        g_in = [sem(f"g_in{s}") for s in range(SLOTS)]
        xg_in = [sem(f"xg_in{h}") for h in range(2)]
        pe_slots = sem("pe_slots")
        acc_step = sem("acc_step")
        acc_zeroed = sem("acc_zeroed")
        xT_in = sem("xT_in")
        xTs_scaled = sem("xTs_scaled")
        y_evac = sem("y_evac")
        deg_ready = sem("deg_ready")
        dve_step = sem("dve_step")
        s_copied = sem("s_copied")
        y_copied = sem("y_copied")
        inv_ready = sem("inv_ready")
        h_ready = sem("h_ready")
        xn_in = sem("xn_in")
        var_ready = sem("var_ready")
        std_ready = sem("std_ready")
        x1_ready = sem("x1_ready")
        x1_out = sem("x1_out")
        ss_ready = sem("ss_ready")
        nrm_ready = sem("nrm_ready")
        u_ready = sem("u_ready")
        ln_ready = sem("ln_ready")
        xt_ready = sem("xt_ready")
        xt_out = sem("xt_out")
        xTp_ready = sem("xTp_ready")
        xTt_ready = sem("xTt_ready")
        proj_ready = sem("proj_ready")
        rows_ready = sem("rows_ready")
        rows_out = sem("rows_out")
        prcr_ready = sem("prcr_ready")

        c_in = [sem(f"c_in{k}") for k in range(3 * CHUNKS)]
        adir_in = [sem(f"adir_in{k}") for k in range(DIR_SLOTS)]
        lI_in = sem("lI_in")
        lJ_in = sem("lJ_in")
        xtI_in = sem("xtI_in")
        xtJ_in = sem("xtJ_in")
        p_ready = sem("p_ready")
        c_ready = sem("c_ready")
        t_ready = sem("t_ready")
        nat_ready = sem("nat_ready")
        dir_used = sem("dir_used")
        turn_used = sem("turn_used")
        kt_ready = sem("kt_ready")
        kt_used = sem("kt_used")
        sup_zeroed = sem("sup_zeroed")
        before_zeroed = sem("before_zeroed")
        evac_done = sem("evac_done")

        x1f_in = [sem(f"x1f_in{h}") for h in range(4)]
        uT_ready = sem("uT_ready")
        u_copied = sem("u_copied")
        s_ready = sem("s_ready")
        pool_scaled = sem("pool_scaled")
        pool_added = sem("pool_added")
        act_sumsq_ready = sem("act_sumsq_ready")
        last_ready = sem("last_ready")
        sq_ready = sem("sq_ready")
        sumsq_ready = sem("sumsq_ready")
        f_dev = sem("f_dev")
        norm_ready = sem("norm_ready")
        f_step = sem("f_step")
        f_norm = sem("f_norm")
        f_act = sem("f_act")
        fvar_ready = sem("fvar_ready")
        o_ready = sem("o_ready")
        out_done = sem("out_done")

        N_CONST = 9

        def constant_wait(eng):
            eng.wait_ge(const_in, 16 * N_CONST)

        def peeled(q):
            return 2 if q == 1 else 1

        block = ctx.enter_context(nc.Block())

        @block.sync
        def _(sp):
            def load_trip(q, t, first=False):
                n = q * TRIPS + t
                for s in range(STEPS):
                    slot, xh = s % SLOTS, (s // 2) % 2
                    fresh = first and s < SLOTS
                    if s % 2 == 0:
                        if not fresh:
                            used = sp.lower_val(n * STEPS + s - 2)
                            constant_wait(sp)
                            sp.wait_ge(pe_slots, used)
                        sp.dma_start(xg[:, xh, :], x_g[t * (STEPS // 2) + s // 2]).then_inc(xg_in[xh], 16)
                    if not fresh:
                        used = sp.lower_val(n * STEPS + s - 3)
                        added = sp.lower_val((n * STEPS + s - 3) * 2)
                        constant_wait(sp)
                        sp.wait_ge(pe_slots, used)
                        sp.wait_ge(acc_step, added)
                    for b in range(BPQ):
                        sp.dma_start(g0[slot][:, b], g_blk[t * 2 + s // SLOTS, q * BPQ + b,
                                                           slot * 2 * P:(slot + 1) * 2 * P, :]
                                     .rearrange("(t p) c -> p t c", p=P)).then_inc(g_in[slot], 16)

            for q in range(NQ):
                if q == 0:
                    load_trip(0, 0, first=True)
                with sp.Fori(1 if q == 0 else 0, TRIPS) as t:
                    load_trip(q, t)

            def load_chunks(it, b, chunks, prev_it=None):
                other = (it + BLOCK_DIST[b]) % NPAN
                src = g_blk[it, other] if b in (X1, X2, X3, X4) else g_blk[other, it]
                for c in chunks:
                    if prev_it is not None:
                        h = holders(b % 3, c)
                        before = h[h.index(b) - 1]
                        trn = phase_of(before, TRN) if turned_chunk(c) else None
                        nat = phase_of(before, NAT)
                        turned = None if trn is None else sp.lower_val(prev_it * UPI + (trn + 1) * UNITS)
                        used = None if nat is None else sp.lower_val(prev_it * UPI + nat * UNITS + 2 * c + 3)
                        constant_wait(sp)
                        if trn is not None:
                            sp.wait_ge(t_ready, turned)
                        if nat is not None:
                            sp.wait_ge(nat_ready, used)
                    k = (b % 3) * CHUNKS + c
                    sp.dma_start(ring[:, k * CH:(k + 1) * CH].rearrange("p (t c) -> p t c", t=2),
                                 src[c * CHUNK_ROWS:(c + 1) * CHUNK_ROWS, :].rearrange("(t p) c -> p t c", p=P)) \
                        .then_inc(c_in[k], 16)

            def load_xt(dst, panel, done):
                sp.dma_start(dst[:, :].rearrange("p (g c) -> p g c", g=BP // GC),
                             xt_d[ds(panel * (BP // GC), BP // GC)].rearrange("g p c -> p g c")).then_inc(done, 16)

            def load_l(dst, panel, done):
                for r in range(2):
                    sp.dma_start(dst[:, r, :], plcl_d[r:r + 1, ds(panel * BP, BP)].to_broadcast([P, BP])) \
                        .then_inc(done, 16)

            sp.wait_ge(pe_slots, NQ * TRIPS * STEPS)
            sp.wait_ge(acc_step, NQ * TRIPS * STEPS * 2)
            for b, groups in ((Y1, NG - 3), (X1, NG)):
                sp.wait_ge(xn_in, groups * 16)
                load_chunks(0, b, range(CHUNKS))
            sp.wait_ge(xt_out, 16 * NG)
            sp.wait_ge(rows_out, 16 * NG)
            sp.wait_ge(y_copied, NG)
            load_l(lJ, 1, lJ_in)
            load_xt(xtJ, 1, xtJ_in)
            load_xt(xtI, 0, xtI_in)
            load_l(lI, 0, lI_in)
            for c in range(CHUNKS):
                sp.wait_ge(c_ready, 2 * c + 2)
                load_chunks(0, DG, [c])

            def next_xt(dst, it, ph, panel, done):
                used = sp.lower_val(it * UPI + (ph + 1) * UNITS + CSIG)
                constant_wait(sp)
                sp.wait_ge(kt_used, used)
                load_xt(dst, panel % NPAN, done)

            def next_l(dst, it, ph, panel, done):
                used = sp.lower_val(it * UPI + (ph + 1) * UNITS)
                constant_wait(sp)
                sp.wait_ge(c_ready, used)
                sp.wait_ge(p_ready, used)
                load_l(dst, panel % NPAN, done)

            def iteration(it, last):
                next_l(lJ, it, 0, it + 2, lJ_in)
                load_chunks(it, X2, range(CHUNKS), it)
                next_xt(xtJ, it, 1, it + 2, xtJ_in)
                load_chunks(it, Y2, range(CHUNKS), it)
                load_chunks(it, Y4, range(CHUNKS), it)
                next_xt(xtJ, it, 3, it + 4, xtJ_in)
                load_chunks(it, X4, range(TURNED_CHUNKS), it)
                next_l(lJ, it, 4, it + 3, lJ_in)
                load_chunks(it, Y3, range(TURNED_CHUNKS), it)
                load_chunks(it, X3, range(CHUNKS), it)
                load_chunks(it, Y3, range(TURNED_CHUNKS, CHUNKS), it)
                next_xt(xtJ, it, 5, it + 3, xtJ_in)
                if last:
                    return
                load_chunks(it + 1, Y1, range(CHUNKS), it)
                next_l(lJ, it, 6, it + 2, lJ_in)
                next_xt(xtI, it, XTI_LAST, it + 1, xtI_in)
                load_chunks(it + 1, X1, range(CHUNKS), it)
                next_l(lI, it, LI_LAST, it + 1, lI_in)
                next_xt(xtJ, it, 7, it + 2, xtJ_in)
                load_chunks(it + 1, DG, range(CHUNKS), it)

            with sp.Fori(0, NPAN - 1) as it:
                iteration(it, False)
            iteration(NPAN - 1, True)

            sp.wait_ge(x1_out, 16 * NG)
            sp.wait_ge(t_ready, LAST * UPI + (phase_of(X4, TRN) + 1) * UNITS)
            sp.wait_ge(nat_ready, LAST * UPI + (phase_of(X2, NAT) + 1) * UNITS + 1)
            for h in range(4):
                g = NG // 4
                sp.dma_start(x1f[:, h * g * GC:(h + 1) * g * GC].rearrange("p (g c) -> p g c", g=g),
                             x1_d[h * g:(h + 1) * g].rearrange("g p c -> p g c")).then_inc(x1f_in[h], 16)
            for i, (p, _) in enumerate(ORDER):
                if i < NPAN - 1:
                    sp.wait_ge(o_ready, i + 1)
                else:
                    sp.wait_ge(last_ready, 1)
                sp.dma_start(out[p * BP:(p + 1) * BP, :].rearrange("(t p) d -> p t d", p=P),
                             res_o[:, p * BP:(p + 1) * BP].rearrange("p (t d) -> p t d", t=TPP)).then_inc(out_done, 16)
            sp.wait_ge(out_done, 16 * NPAN)

        @block.gpsimd
        def _(pool):
            pool.memset(ones[:, :], 1.0).then_inc(ident_ready, 1)
            pool.memset(epsc[:, :], LN_EPS).then_inc(ident_ready, 1)
            pool.memset(ident[:, :], 0.0).then_inc(ident_ready, 1)
            pool.wait_ge(ident_ready, 3)
            pool.affine_select(out=ident[:, :], in_=ident[:, :], compare_op=ALU.not_equal, fill=1.0, base=0,
                               pattern=[[-1, P]], channel_multiplier=1).then_inc(ident_ready, 1)
            pool.sem_inc(turn_used, TBUF)
            pool.sem_inc(dir_used, DIR_CREDIT)
            pool.sem_inc(nat_ready, 1)
            pool.sem_inc(kt_ready, PSIG - 1)
            pool.sem_inc(kt_used, CSIG - LAG)
            pool.sem_inc(evac_done, 1)

            for q in range(NQ):
                if q >= 2:
                    pool.wait_ge(s_copied, GPQ * (q - 1))
                pool.memset(accS[:, q % 2, :], 0.0).then_inc(acc_zeroed, 1)

            pool.wait_ge(s_copied, NG)
            pool.wait_ge(pe_slots, NQ * TRIPS * STEPS)
            pool.memset(acc[:, :], 0.0).then_inc(sup_zeroed, 1)
            pool.wait_ge(rows_out, 16 * NG)
            pool.wait_ge(xt_out, 16 * NG)
            pool.wait_ge(x1_out, 16 * NG)
            pool.wait_ge(proj_ready, NG)
            pool.wait_ge(prcr_ready, NG)
            pool.memset(csig[:, CSIG - LAG:CSIG, :], 0.0).then_inc(before_zeroed, 1)
            pool.memset(psig[:, PSIG - 1, :], 0.0).then_inc(before_zeroed, 1)

            with pool.Fori(0, NPAN) as it:
                for ph in range(PHASES):
                    blk = PH[ph][NAT]
                    for u in range(UNITS):
                        n = ph * UNITS + u
                        k = (blk % 3) * CHUNKS + u // 2
                        if u % 2 == 0:
                            pool.wait_ge(c_in[k], arrivals(it, blk, u // 2) * 16)
                        pool.wait_ge(p_ready, it * UPI + n + 1)
                        pool.tensor_tensor(out=psig[:, n % PSIG, :], in0=psig[:, n % PSIG, :],
                                           in1=ring[:, k * CH + (u % 2) * BP:k * CH + (u % 2 + 1) * BP],
                                           op=ALU.mult).then_inc(nat_ready, 1)

            pool.wait_ge(s_ready, 1)
            for h in range(4):
                pool.wait_ge(x1f_in[h], 16)
            for i, (p, _) in enumerate(ORDER):
                pool.wait_ge(u_copied, (i + 1) * GPP)
                tiles = slice((p + 1) * TPP - BY_POOL, (p + 1) * TPP)
                u = uN[:, tiles.start * D:tiles.stop * D]
                u3 = u.rearrange("p (t d) -> p t d", t=BY_POOL)
                pool.tensor_tensor(out=u3, in0=u3, in1=s_s[:, tiles].unsqueeze(2).to_broadcast([P, BY_POOL, D]),
                                   op=ALU.mult).then_inc(pool_scaled, 1)
                pool.wait_ge(pool_scaled, i + 1)
                ins = pool.tensor_tensor(out=u, in0=u, in1=x1f[:, tiles.start * D:tiles.stop * D], op=ALU.add)
                ins.then_inc(pool_added, 1)

        @block.scalar
        def _(act):
            def load_xT(q):
                if q >= 2:
                    act.wait_ge(y_copied, GPQ * (q - 1))
                act.dma_start(yS[:, q % 2, :], xT[:, q * QC:(q + 1) * QC]).then_inc(xT_in, 16)
                act.wait_ge(xT_in, 16 * (q + 1))
                if q == 0:
                    act.wait_ge(oma_ready, 1)
                act.activation(yS[:, q % 2, :], yS[:, q % 2, :], ACT.Copy, scale=oma[:, 0:1]).then_inc(xTs_scaled, 1)

            def stage_group(q, t, first):
                G = (q - 1) * GPQ + t
                if first:
                    act.wait_ge(acc_step, q * TRIPS * STEPS * 2)
                used = act.lower_val(G)
                constant_wait(act)
                act.wait_ge(deg_ready, used)
                act.activation(s_st, accS[:, (q - 1) % 2, ds(t * GC, GC)], ACT.Copy).then_inc(s_copied, 1)
                if first:
                    act.wait_ge(y_evac, q)
                constant_wait(act)
                act.wait_ge(h_ready, used)
                act.activation(y_st, yS[:, (q - 1) % 2, ds(t * GC, GC)], ACT.Copy).then_inc(y_copied, 1)
                act.wait_ge(var_ready, G)
                act.dma_start(xn, x_g[G]).then_inc(xn_in, 16)

            def logarithm(G):
                act.wait_ge(u_ready, G + 1)
                act.activation(lnu, uu, ACT.Ln).then_inc(ln_ready, 1)

            def tangent_out(G):
                act.wait_ge(xt_ready, G + 1)
                act.dma_start(xt_d[G], xt_st).then_inc(xt_out, 16)
                act.wait_ge(xTp_ready, G + 1)
                act.wait_ge(proj_ready, G)
                act.activation(xTt, ps_e()[:, 2 * BANK:2 * BANK + GC], ACT.Copy).then_inc(xTt_ready, 1)

            def deviation(G):
                act.wait_ge(var_ready, G + 1)
                act.activation(std, mv[:, :, 1], ACT.Sqrt, bias=epsc[:, 0:1]).then_inc(std_ready, 1)

            def norms(G):
                act.wait_ge(x1_ready, G + 1)
                act.dma_start(x1_d[G], x1b).then_inc(x1_out, 16)
                for k in range(GT):
                    ins = act.activation(junk[:, k * D:(k + 1) * D], x1b[:, k * D:(k + 1) * D], ACT.Square,
                                         accum_out=ss[:, k:k + 1])
                ins.then_inc(ss_ready, 1)
                act.wait_ge(ss_ready, G + 1)
                act.activation(nrm, ss, ACT.Sqrt).then_inc(nrm_ready, 1)

            def rows_to_dram(G):
                act.wait_ge(proj_ready, G + 1)
                act.wait_ge(rows_out, G * 16)
                act.activation(rows, ps_e()[0:2, 3 * BANK:3 * BANK + GC], ACT.Copy).then_inc(rows_ready, 1)
                act.wait_ge(rows_ready, G + 1)
                act.dma_start(plcl_d[:, ds(G * GC, GC)], rows).then_inc(rows_out, 16)

            def trip(q, t, prev, first=False, last=False):
                G = (q - 1) * GPQ + t
                if q < NQ or first:
                    stage_group(q, t, first)
                if q == NQ:
                    deviation(G)
                    if not last:
                        stage_group(q, t + 1, False)
                if prev:
                    logarithm(G - 1)
                    tangent_out(G - 1)
                if q < NQ:
                    deviation(G)
                norms(G)
                if prev:
                    rows_to_dram(G - 1)

            def ps_e():
                return ps[ep_set[0]]

            for dst, src in (
                (WTs[:, :], WT), (bb[:, :], b_row.rearrange("(a d) -> a d", a=1).to_broadcast([P, D])),
                (alph[:, :], alpha.rearrange("(a d) -> a d", a=1).to_broadcast([P, 1])),
                (bpc[:, 0:1], b_par.rearrange("(a d) -> a d", a=1).to_broadcast([P, 1])),
                (bpc[:, 1:2], b_chi.rearrange("(a d) -> a d", a=1).to_broadcast([P, 1])),
                (wl[:, 0:1], w_par[0:D].rearrange("(d a) -> d a", a=1)),
                (wl[:, 1:2], w_chi[0:D].rearrange("(d a) -> d a", a=1)),
                (wr[:, 0:1], w_par[D:2 * D].rearrange("(d a) -> d a", a=1)),
                (wr[:, 1:2], w_chi[D:2 * D].rearrange("(d a) -> d a", a=1)),
            ):
                act.dma_start(dst, src).then_inc(const_in, 16)

            ep_set = [0]
            act.wait_ge(ident_ready, 4)
            load_xT(0)
            for q in range(1, NQ + 1):
                ep_set[0] = (q - 1) % 2
                for t in range(peeled(q)):
                    trip(q, t, prev=(q, t) != (1, 0), first=t == 0)
                if q < NQ:
                    load_xT(q)
                with act.Fori(peeled(q), GPQ - 1) as t:
                    trip(q, t, prev=True)
                trip(q, GPQ - 1, prev=True, last=True)
            logarithm(NG - 1)
            tangent_out(NG - 1)
            rows_to_dram(NG - 1)

            act.wait_ge(rows_out, 16 * NG)
            act.wait_ge(xt_out, 16 * NG)
            act.wait_ge(x1_out, 16 * NG)
            act.wait_ge(proj_ready, NG)
            act.wait_ge(prcr_ready, NG)
            act.wait_ge(ss_ready, NG)
            act.preload_act_table(ACT.Sigmoid)

            def load_direct(it, n, fresh=False):
                later, n = divmod(n, UPI)
                ph, u = divmod(n, UNITS)
                slot = n // 2 % DIR_SLOTS
                if not fresh:
                    used = act.lower_val((it + later) * UPI + n + 2 - 2 * DIR_SLOTS + DIR_CREDIT)
                    constant_wait(act)
                    act.wait_ge(dir_used, used)
                i, j = (it + later) % NPAN, (it + later + PH[ph][DIST]) % NPAN
                src = a_cols[i, j] if PH[ph][TO_J] else a_cols[j, i]
                act.dma_start(adir[:, slot], src[u * P:(u + 2) * P, :].rearrange("(t p) c -> p t c", p=P)) \
                    .then_inc(adir_in[slot], 16)

            for n in range(0, AHEAD, 2):
                load_direct(0, n, fresh=True)
            with act.Fori(0, NPAN) as it:
                for ph in range(PHASES):
                    _, _, dist, to_j, _ = PH[ph]
                    cols = lJ if to_j else lI
                    tile0 = it * TPP if to_j or dist == 0 else ((it + dist) % NPAN) * TPP
                    if to_j:
                        act.wait_ge(lJ_in, (it * len(LJ_PHASES) + LJ_PHASES.index(ph) + 1) * 32)
                    elif ph == LI_FIRST:
                        act.wait_ge(lI_in, (it + 1) * 32)
                    for u in range(UNITS):
                        n = ph * UNITS + u
                        if n % 2 == 0:
                            load_direct(it, n + AHEAD)
                        free = act.lower_val(it * UPI + n + 1)
                        constant_wait(act)
                        act.wait_ge(kt_ready, free)
                        act.activation(psig[:, n % PSIG, :], cols[:, 0, :], ACT.Sigmoid,
                                       bias=prcr[:, ds((tile0 + u) * 2, 1)]).then_inc(p_ready, 1)
                        constant_wait(act)
                        act.wait_ge(kt_used, free)
                        act.activation(csig[:, n % CSIG, :], cols[:, 1, :], ACT.Sigmoid,
                                       bias=prcr[:, ds((tile0 + u) * 2 + 1, 1)]).then_inc(c_ready, 1)

            for n in range(0, AHEAD, 2):
                act.wait_ge(adir_in[n // 2], (NPAN * DIR_LOADS + 1) * 16)
            act.preload_act_table(ACT.Sqrt)
            act.wait_ge(c_ready, NPAN * UPI)
            act.wait_ge(p_ready, NPAN * UPI)
            for i, (p, evacs) in enumerate(NORM_BY_PE):
                act.wait_ge(evac_done, LAST * EVACS + evacs + 1)
                act.activation(squares[i], acc[:, p * BP:(p + 1) * BP], ACT.Square).then_inc(sq_ready, 1)
            act.wait_ge(nat_ready, NPAN * UPI + 1)
            act.wait_ge(t_ready, NPAN * UPI)
            for i, (p, _) in enumerate(NORM_BY_ACT):
                for g in range(GPP):
                    act.wait_ge(u_copied, i * GPP + g + 1)
                    for k in range(p * TPP + g * (BANK // D), p * TPP + (g + 1) * (BANK // D)):
                        ins = act.activation(res_o[:, k * D:(k + 1) * D], uN[:, k * D:(k + 1) * D],
                                             ACT.Square, accum_out=s_ss[:, k:k + 1])
                ins.then_inc(act_sumsq_ready, 1)
            act.wait_ge(sumsq_ready, 1)
            act.activation(s_n[:, PE_TILES], sumsq[:, PE_TILES], ACT.Sqrt).then_inc(f_norm, 1)
            act.wait_ge(act_sumsq_ready, len(NORM_BY_ACT))
            for p, _ in NORM_BY_ACT:
                tiles = slice(p * TPP, (p + 1) * TPP)
                act.activation(s_n[:, tiles], s_ss[:, tiles], ACT.Sqrt).then_inc(f_norm, 1)
            act.wait_ge(f_step, 1)
            act.activation(s_th, s_nm, ACT.Tanh).then_inc(f_act, 1)
            act.preload_act_table(ACT.Sqrt)

            def normalised(i):
                p, _ = ORDER[i]
                act.wait_ge(norm_ready, i + 1)
                for k in range(p * TPP, (p + 1) * TPP):
                    ins = act.activation(res_o[:, k * D:(k + 1) * D], uN[:, k * D:(k + 1) * D], ACT.Identity,
                                         bias=s_mb[:, k:k + 1], scale=s_rs[:, k:k + 1])
                ins.then_inc(o_ready, 1)

            for i, (p, _) in enumerate(ORDER):
                tiles = slice(p * TPP, (p + 1) * TPP)
                act.wait_ge(fvar_ready, i + 1)
                act.activation(s_sd[:, tiles], mvf[:, tiles, 1], ACT.Sqrt, bias=epsc[:, 0:1]).then_inc(f_dev, 1)
                if i > 0:
                    normalised(i - 1)

        @block.vector
        def _(dve):
            steps = [0]

            def step(base, ins):
                steps[0] += 1
                ins.then_inc(dve_step, 1)
                dve.wait_ge(dve_step, base + steps[0])

            dve.wait_ge(const_in, 16 * N_CONST)
            dve.tensor_scalar(oma[:, :], alph[:, :], -1.0, 1.0, ALU.mult, ALU.add).then_inc(oma_ready, 1)
            dve.wait_ge(oma_ready, 1)

            def add_slot(q, t, s):
                m = (q * TRIPS + t) * STEPS + s
                dve.wait_ge(g_in[s % SLOTS], ((q * TRIPS + t) * 2 + s // SLOTS + 1) * 32)
                for tt in range(2):
                    dst = accS[:, q % 2, :].rearrange("p (b c) -> p b c", b=BPQ)
                    dve.tensor_tensor(out=dst, in0=dst, in1=g0[s % SLOTS][:, :, tt, :], op=ALU.add).then_inc(acc_step, 1)
                    dve.wait_ge(acc_step, m * 2 + tt + 1)

            def inverse_degrees(q, t, base):
                E = ps[(q - 1) % 2]
                G = (q - 1) * GPQ + t
                dve.wait_ge(deg_ready, G + 1)
                step(base, dve.tensor_scalar(dg, E[:, 0:GT], alph[:, 0:1], oma[:, 0:1], ALU.mult, ALU.add))
                step(base, dve.scalar_tensor_tensor(out=sf, in0=dg, scalar=0.0, in1=dg, op0=ALU.is_equal, op1=ALU.add))
                step(base, dve.reciprocal(rc, sf))
                dve.scalar_tensor_tensor(out=inv, in0=dg, scalar=0.0, in1=rc, op0=ALU.not_equal, op1=ALU.mult) \
                    .then_inc(inv_ready, 1)

            def log_map_argument(G, base):
                dve.wait_ge(nrm_ready, G + 1)
                step(base, dve.tensor_scalar(nrm2, nrm, MIN_NORM, None, ALU.max))
                step(base, dve.tensor_scalar(clp, nrm2, CLIP, None, ALU.min))
                step(base, dve.tensor_scalar(om, clp, -1.0, 1.0, ALU.mult, ALU.add))
                step(base, dve.reciprocal(rom, om))
                step(base, dve.scalar_tensor_tensor(out=tt2, in0=clp, scalar=2.0, in1=rom, op0=ALU.mult, op1=ALU.mult))
                dve.tensor_scalar(uu, tt2, 1.0, None, ALU.add).then_inc(u_ready, 1)

            def log_map_factor(G, base):
                dve.wait_ge(ln_ready, G + 1)
                step(base, dve.tensor_scalar(um1, uu, -1.0, None, ALU.add))
                step(base, dve.tensor_scalar(zz, um1, 0.0, None, ALU.is_equal))
                step(base, dve.tensor_tensor(out=ums, in0=um1, in1=zz, op=ALU.add))
                step(base, dve.reciprocal(um1, ums))
                step(base, dve.tensor_tensor(out=ums, in0=lnu, in1=um1, op=ALU.mult))
                step(base, dve.tensor_tensor(out=ums, in0=ums, in1=zz, op=ALU.add))
                step(base, dve.scalar_tensor_tensor(out=l1p, in0=ums, scalar=0.5, in1=tt2, op0=ALU.mult, op1=ALU.mult))
                step(base, dve.reciprocal(um1, nrm2))
                step(base, dve.tensor_tensor(out=fac, in0=l1p, in1=um1, op=ALU.mult))
                dve.wait_ge(xTp_ready, G)
                dve.wait_ge(xt_out, G * 16)
                for k in range(GT):
                    ins = dve.tensor_scalar(xt_st[:, k * D:(k + 1) * D], x1b[:, k * D:(k + 1) * D], fac[:, k:k + 1],
                                            None, ALU.mult)
                ins.then_inc(xt_ready, 1)

            def residual_stats(q, t, base):
                E = ps[(q - 1) % 2]
                G = (q - 1) * GPQ + t
                dve.wait_ge(h_ready, G + 1)
                dve.wait_ge(inv_ready, G + 1)
                for k in range(GT):
                    ins = dve.scalar_tensor_tensor(out=r_st[:, k * D:(k + 1) * D],
                                                   in0=E[:, BANK + k * D:BANK + (k + 1) * D],
                                                   scalar=inv[:, k:k + 1], in1=bb[:, :], op0=ALU.mult, op1=ALU.add)
                dve.wait_ge(xn_in, (G + 1) * 16)
                step(base, ins)
                step(base, dve.scalar_tensor_tensor(out=r_st, in0=r_st, scalar=0.0, in1=xn,
                                                    op0=ALU.max, op1=ALU.add))
                for k in range(GT):
                    ins = dve.bn_stats(bst[:, k, :], r_st[:, k * D:(k + 1) * D])
                steps[0] += 1
                ins.then_inc(dve_step, 1)
                stats = dve.lower_val(base + steps[0])
                constant_wait(dve)
                dve.wait_ge(dve_step, stats)
                for k in range(GT):
                    ins = dve.bn_aggr(mv[:, k, :], bst[:, k, :])
                ins.then_inc(var_ready, 1)

            def normalise(G, base):
                dve.wait_ge(std_ready, G + 1)
                step(base, dve.reciprocal(rstd, std))
                dve.wait_ge(x1_out, G * 16)
                for k in range(GT):
                    ins = dve.tensor_scalar(x1b[:, k * D:(k + 1) * D], r_st[:, k * D:(k + 1) * D],
                                            mv[:, k, 0:1], rstd[:, k:k + 1], ALU.subtract, ALU.mult)
                ins.then_inc(x1_ready, 1)

            def row_biases(q, G):
                E = ps[(q - 1) % 2]
                dve.wait_ge(proj_ready, G + 1)
                dve.tensor_tensor(out=prcr[:, ds(G * GT * 2, GT * 2)],
                                  in0=E[:, 2 * BANK:2 * BANK + 2 * GT], in1=bpc2[:, :], op=ALU.add) \
                    .then_inc(prcr_ready, 1)

            def trip(q, t, prev, base, first=False):
                main = q < NQ
                epi = q > 0
                G = (q - 1) * GPQ + t
                if not main:
                    inverse_degrees(q, t, base)
                    residual_stats(q, t, base)
                    if not first:
                        row_biases(q, G - 2)
                    log_map_argument(G - 1, base)
                    log_map_factor(G - 1, base)
                    normalise(G, base)
                    return
                if prev:
                    log_map_argument(G - 1, base)
                if epi:
                    inverse_degrees(q, t, base)
                if prev and first:
                    log_map_factor(G - 1, base)
                add_slot(q, t, 0)
                add_slot(q, t, 1)
                if prev and not first:
                    log_map_factor(G - 1, base)
                if epi:
                    residual_stats(q, t, base)
                add_slot(q, t, 2)
                add_slot(q, t, 3)
                if epi:
                    normalise(G, base)
                add_slot(q, t, 4)
                add_slot(q, t, 5)
                if prev:
                    row_biases(q, G - 1)
                add_slot(q, t, 6)
                add_slot(q, t, 7)

            for k in range(GT):
                dve.tensor_copy(bpc2[:, 2 * k:2 * k + 2], bpc[:, :]).then_inc(bpc2_ready, 1)
            dve.wait_ge(bpc2_ready, GT)
            for q in range(NQ + 1):
                if q < NQ:
                    dve.wait_ge(acc_zeroed, q + 1)
                if q > 0:
                    dve.wait_ge(pe_slots, q * TRIPS * STEPS)
                    dve.wait_ge(xTs_scaled, q)
                    yq = yS[:, (q - 1) % 2, :]
                    dve.scalar_tensor_tensor(out=yq, in0=ps[(q - 1) % 2][:, :], scalar=alph[:, 0:1], in1=yq,
                                             op0=ALU.mult, op1=ALU.add).then_inc(y_evac, 1)
                    dve.wait_ge(y_evac, q)
                for t in range(peeled(q)):
                    trip(q, t, prev=q > 0 and (q, t) != (1, 0), base=0, first=t == 0)
                before = steps[0]
                with dve.Fori(peeled(q), TRIPS) as t:
                    count = STEPS_PER_TRIP if q > 0 else 0
                    trip(q, t, prev=q > 0, base=(t - peeled(q)) * count)
                assert steps[0] - before == count
                steps[0] = before + (TRIPS - peeled(q)) * count
            row_biases(NQ, NG - 2)
            log_map_argument(NG - 1, 0)
            log_map_factor(NG - 1, 0)
            row_biases(NQ, NG - 1)

            def evacuate(products_done, evacs_before, ph, panel):
                dve.wait_ge(kt_used, products_done + CSIG)
                dve.wait_ge(evac_done, evacs_before + 1)
                dst = acc[:, ds(panel * BP, BP)]
                dve.tensor_tensor(out=dst, in0=OUTP[PH[ph][OUT]], in1=dst, op=ALU.add).then_inc(evac_done, 1)

            dve.wait_ge(sup_zeroed, 1)
            def turned_product(it, n):
                kt = csig[:, n % CSIG, :]
                slot = n // 2 % DIR_SLOTS
                dve.wait_ge(c_ready, it * UPI + n + 1)
                dve.wait_ge(adir_in[slot], (it * DIR_LOADS + n // 2 // DIR_SLOTS + 1) * 16)
                dve.tensor_tensor(out=kt[:, TURNED:BP], in0=adir[:, slot, n % 2, :], in1=kt[:, TURNED:BP],
                                  op=ALU.mult).then_inc(dir_used, 1)
                dve.wait_ge(t_ready, it * UPI + n + 1)
                dve.tensor_tensor(out=kt[:, 0:TURNED], in0=TP[n % TBUF][:, 0:TURNED], in1=kt[:, 0:TURNED],
                                  op=ALU.mult).then_inc(turn_used, 1)

            def sums(it, n):
                dve.wait_ge(dir_used, it * UPI + n + 1 + DIR_CREDIT)
                dve.wait_ge(turn_used, it * UPI + n + 1 + TBUF)
                dve.wait_ge(nat_ready, it * UPI + n + 2)
                dve.tensor_tensor(out=csig[:, n % CSIG, :], in0=csig[:, n % CSIG, :], in1=psig[:, n % PSIG, :],
                                  op=ALU.add).then_inc(kt_ready, 1)

            dve.wait_ge(before_zeroed, 2)
            with dve.Fori(0, NPAN) as it:
                for ph in range(PHASES):
                    for u in range(UNITS):
                        n = ph * UNITS + u
                        turned_product(it, n)
                        sums(it, n - 1)
                        for e, (of, during) in enumerate(EVAC):
                            if (ph, u) == (during, LAG + 1):
                                if of == 7:
                                    evacuate(it * UPI, it * EVACS + e, of, (it + NPAN - 1) % NPAN)
                                else:
                                    to = (it + PH[of][DIST]) % NPAN if PH[of][TO_J] else it
                                    evacuate(it * UPI + (of + 1) * UNITS, it * EVACS + e, of, to)
            sums(NPAN, -1)
            evacuate(NPAN * UPI, NPAN * EVACS, 7, NPAN - 1)

            dve.wait_ge(t_ready, NPAN * UPI)
            dve.wait_ge(nat_ready, NPAN * UPI + 1)
            def copy_group(g):
                dve.wait_ge(uT_ready, g + 1)
                dve.tensor_copy(group_of_u(g), ps[0][:, (g % 4) * BANK:(g % 4 + 1) * BANK]).then_inc(u_copied, 1)

            for g in range(9):
                copy_group(g)
            dve.wait_ge(f_norm, 1 + len(NORM_BY_ACT))
            dve.tensor_scalar(s_nm, s_n, MIN_NORM, None, ALU.max).then_inc(f_step, 1)
            dve.wait_ge(f_step, 1)
            step(0, dve.reciprocal(s_rn, s_nm))
            for g in range(9, N // BANK):
                copy_group(g)
            dve.wait_ge(f_act, 1)
            step(0, dve.tensor_tensor(out=s_s1, in0=s_th, in1=s_rn, op=ALU.mult))
            step(0, dve.tensor_tensor(out=s_n2, in0=s_s1, in1=s_n, op=ALU.mult))
            step(0, dve.tensor_scalar(s_n2, s_n2, MIN_NORM, None, ALU.max))
            step(0, dve.reciprocal(s_s, s_n2))
            step(0, dve.tensor_scalar(s_s, s_s, MAXNORM, 1.0, ALU.mult, ALU.min))
            dve.tensor_tensor(out=s_s, in0=s_s1, in1=s_s, op=ALU.mult).then_inc(s_ready, 1)
            dve.wait_ge(s_ready, 1)
            dve.wait_ge(u_copied, N // BANK)

            def norm_factors(i):
                p, _ = ORDER[i]
                tiles = slice(p * TPP, (p + 1) * TPP)
                dve.wait_ge(f_dev, i + 1)
                step(0, dve.reciprocal(s_rs[:, tiles], s_sd[:, tiles]))
                dve.scalar_tensor_tensor(out=s_mb[:, tiles], in0=mvf[:, tiles, 0], scalar=-1.0, in1=s_rs[:, tiles],
                                         op0=ALU.mult, op1=ALU.mult).then_inc(norm_ready, 1)

            for h in range(4):
                dve.wait_ge(x1f_in[h], 16)
            for i, (p, _) in enumerate(ORDER):
                tiles = range(p * TPP, (p + 1) * TPP)
                for k in tiles[:TPP - BY_POOL]:
                    ins = dve.scalar_tensor_tensor(out=uN[:, k * D:(k + 1) * D], in0=uN[:, k * D:(k + 1) * D],
                                                   scalar=s_s[:, k:k + 1], in1=x1f[:, k * D:(k + 1) * D],
                                                   op0=ALU.mult, op1=ALU.add)
                step(0, ins)
                dve.wait_ge(pool_added, i + 1)
                for k in tiles:
                    ins = dve.bn_stats(bstf[:, k, :], uN[:, k * D:(k + 1) * D])
                step(0, ins)
                for k in tiles:
                    ins = dve.bn_aggr(mvf[:, k, :], bstf[:, k, :])
                ins.then_inc(fvar_ready, 1)
                if i > 0:
                    norm_factors(i - 1)
            p, _ = ORDER[-1]
            tiles = slice(p * TPP, (p + 1) * TPP)
            dve.wait_ge(f_dev, NPAN)
            step(0, dve.reciprocal(s_rs[:, tiles], s_sd[:, tiles]))
            for k in range(p * TPP, (p + 1) * TPP):
                ins = dve.tensor_scalar(res_o[:, k * D:(k + 1) * D], uN[:, k * D:(k + 1) * D],
                                        mvf[:, k, 0:1], s_rs[:, k:k + 1], ALU.subtract, ALU.mult)
            ins.then_inc(last_ready, 1)

        @block.tensor
        def _(pe):
            def main_step(q, t, s, first, last):
                n = (q * TRIPS + t) * 2 + s // SLOTS
                slot, xh = s % SLOTS, (s // 2) % 2
                if s % 2 == 0:
                    pe.wait_ge(xg_in[xh], (n + 1) * 16)
                pe.wait_ge(g_in[slot], (n + 1) * 32)
                for tt in range(2):
                    lhs = xg[:, xh, ((s % 2) * 2 + tt) * D:((s % 2) * 2 + tt + 1) * D]
                    for b in range(BPQ):
                        for h in range(BP // BANK):
                            k = b * (BP // BANK) + h
                            ins = pe.matmul(ps[q % 2][:, k * BANK:(k + 1) * BANK], lhs,
                                            g0[slot][:, b, tt, h * BANK:(h + 1) * BANK],
                                            start=(first and s == 0 and tt == 0),
                                            stop=(last and s == STEPS - 1 and tt == 1))
                ins.then_inc(pe_slots, 1)

            def degree_sums(q, t):
                G = (q - 1) * GPQ + t
                pe.wait_ge(s_copied, G + 1)
                pe.wait_ge(inv_ready, G)
                for k in range(GT):
                    ins = pe.matmul(ps[(q - 1) % 2][:, k:k + 1], s_st[:, k * P:(k + 1) * P], ones[:, 0:1],
                                    start=True, stop=True)
                ins.then_inc(deg_ready, 1)

            def linear(q, t):
                E = ps[(q - 1) % 2]
                G = (q - 1) * GPQ + t
                pe.wait_ge(y_copied, G + 1)
                pe.wait_ge(var_ready, G)
                for k in range(GT):
                    ins = pe.matmul(E[:, BANK + k * D:BANK + (k + 1) * D], y_st[:, k * P:(k + 1) * P], WTs[:, :],
                                    start=True, stop=True)
                ins.then_inc(h_ready, 1)

            def turn_tangent(q, G):
                E = ps[(q - 1) % 2]
                pe.wait_ge(xt_ready, G + 1)
                pe.wait_ge(xTt_ready, G)
                pe.wait_ge(prcr_ready, G)
                for k in range(GT):
                    ins = pe.transpose(E[:, 2 * BANK + k * P:2 * BANK + (k + 1) * P], xt_st[:, k * D:(k + 1) * D],
                                       ident[:, :])
                ins.then_inc(xTp_ready, 1)

            def projections(q, G):
                E = ps[(q - 1) % 2]
                pe.wait_ge(xTt_ready, G + 1)
                pe.wait_ge(rows_ready, G)
                pe.matmul(E[0:2, 3 * BANK:3 * BANK + GC], wl[:, :], xTt, start=True, stop=True)
                for k in range(GT):
                    ins = pe.matmul(E[:, 2 * BANK + 2 * k:2 * BANK + 2 * k + 2], xTt[:, k * P:(k + 1) * P],
                                    wr[:, :], start=True, stop=True)
                ins.then_inc(proj_ready, 1)

            def trip(q, t, prev, first=False, last=False):
                main = q < NQ
                epi = q > 0
                G = (q - 1) * GPQ + t
                if not main:
                    for ahead in ([0] if first else []) + ([] if last else [1]):
                        degree_sums(q, t + ahead)
                        linear(q, t + ahead)
                    turn_tangent(q, G - 1)
                    projections(q, G - 1)
                    return
                if first:
                    main_step(q, t, 0, first, last)
                if epi:
                    if first:
                        pe.wait_ge(y_evac, q)
                    degree_sums(q, t)
                if not first:
                    main_step(q, t, 0, first, last)
                main_step(q, t, 1, first, last)
                if epi:
                    linear(q, t)
                if prev:
                    turn_tangent(q, G - 1)
                main_step(q, t, 2, first, last)
                main_step(q, t, 3, first, last)
                if prev:
                    projections(q, G - 1)
                main_step(q, t, 4, first, last)
                main_step(q, t, 5, first, last)
                main_step(q, t, 6, first, last)
                main_step(q, t, 7, first, last)

            for q in range(NQ + 1):
                if q == 1:
                    pe.wait_ge(const_in, 16 * N_CONST)
                    pe.wait_ge(ident_ready, 4)
                if q == NQ:
                    pe.wait_ge(y_evac, q)
                if 2 <= q < NQ:
                    pe.wait_ge(inv_ready, (q - 1) * GPQ)
                    pe.wait_ge(var_ready, (q - 1) * GPQ)
                    pe.wait_ge(rows_ready, (q - 1) * GPQ - 1)
                    pe.wait_ge(prcr_ready, (q - 1) * GPQ - 1)
                for t in range(peeled(q)):
                    trip(q, t, prev=q > 0 and (q, t) != (1, 0), first=t == 0)
                with pe.Fori(peeled(q), TRIPS - 1) as t:
                    trip(q, t, prev=q > 0)
                trip(q, TRIPS - 1, prev=q > 0, last=True)
            turn_tangent(NQ, NG - 1)
            projections(NQ, NG - 1)

            def transposes(it, ph, u):
                n = ph * UNITS + u
                blk = PH[ph][TRN]
                if u == 0:
                    for c in range(TURNED_CHUNKS):
                        pe.wait_ge(c_in[(blk % 3) * CHUNKS + c], arrivals(it, blk, c) * 16)
                pe.wait_ge(turn_used, it * UPI + n + 1)
                for v in range(TURNED // P):
                    at = ((blk % 3) * CHUNKS + v // 2) * CH + (v % 2) * BP + u * P
                    ins = pe.transpose(TP[n % TBUF][:, v * P:(v + 1) * P], ring[:, at:at + P], ident[:, :])
                ins.then_inc(t_ready, 1)

            def products(it, n):
                ph, u = divmod(n % UPI, UNITS)
                _, _, dist, to_j, o = PH[ph]
                from_i = to_j or dist == 0
                if u == 0:
                    if from_i:
                        pe.wait_ge(xtI_in, (it + 1) * 16)
                    else:
                        pe.wait_ge(xtJ_in, (it * len(XTJ_PHASES) + XTJ_PHASES.index(ph) + 1) * 16)
                    if o == 1 or ph == OUT_A_FIRST:
                        pe.wait_ge(evac_done, it * EVACS + sum(during < ph for _, during in EVAC) + 1)
                pe.wait_ge(kt_ready, it * UPI + n + 1 + PSIG)
                xt = xtI if from_i else xtJ
                for h in range(BP // BANK):
                    ins = pe.matmul(OUTP[o][:, h * BANK:(h + 1) * BANK], xt[:, u * D:(u + 1) * D],
                                    csig[:, n % CSIG, h * BANK:(h + 1) * BANK],
                                    start=(u == 0 and (o == 1 or ph == OUT_A_FIRST)),
                                    stop=(u == UNITS - 1 and (o == 1 or ph == OUT_A_LAST)))
                ins.then_inc(kt_used, 1)

            pe.wait_ge(rows_ready, NG)
            pe.wait_ge(prcr_ready, NG)
            pe.wait_ge(before_zeroed, 1)
            zeros = csig[:, CSIG - LAG, :]
            for h in range(BP // BANK):
                pe.matmul(OUTP[0][:, h * BANK:(h + 1) * BANK], zeros[:, 0:P], zeros[:, 0:BANK], start=True, stop=False)
            pe.wait_ge(xtJ_in, 16)
            with pe.Fori(0, NPAN) as it:
                for n in range(UPI):
                    transposes(it, n // UNITS, n % UNITS)
                    products(it, n - LAG)
            for n in range(UPI - LAG, UPI):
                products(NPAN - 1, n)

            def turn_group(g):
                panel, evacs = ORDER[g // GPP]
                pe.wait_ge(evac_done, LAST * EVACS + evacs + 1)
                if g >= 4:
                    pe.wait_ge(u_copied, g - 3)
                for k in range(BANK // D):
                    at = panel * BP + g % GPP * BANK + k * P
                    ins = pe.transpose(ps[0][:, (g % 4) * BANK + k * D:(g % 4) * BANK + (k + 1) * D],
                                       acc[:, at:at + P], ident[:, :])
                ins.then_inc(uT_ready, 1)

            pe.wait_ge(turn_used, NPAN * UPI + TBUF)
            for g in range(4):
                turn_group(g)
            pe.wait_ge(evac_done, LAST * EVACS + EVACS + 1)
            for i, (panel, _) in enumerate(NORM_BY_PE):
                pe.wait_ge(sq_ready, i + 1)
                for k in range(TPP):
                    tile = panel * TPP + k
                    ins = pe.matmul(sumsq[:, tile:tile + 1], squares[i][:, k * P:(k + 1) * P], ones[:, 0:1],
                                    start=True, stop=True)
                    if k % 4 == 3 and i < 3:
                        if i == 2 and k == 7:
                            continue
                        turn_group(4 + 2 * i + k // 4)
            ins.then_inc(sumsq_ready, 1)
            for g in range(9, N // BANK):
                turn_group(g)


def kernel(x, adj, L0_gnn_t, L0_gnn_alpha, L0_gnn_W, L0_gnn_b, L1_gnn_w_par, L1_gnn_b_par, L1_gnn_w_chi, L1_gnn_b_chi):
    import numpy as np
    import concourse.bacc as bacc
    from concourse.bass_utils import run_bass_kernel_spmd

    x, adj = np.asarray(x), np.asarray(adj)
    arrays = {
        "x_g": x.reshape(NG, GT, P, D).transpose(0, 2, 1, 3).reshape(NG, P, GC),
        "xT": x.T,
        "g_blk": adj.T.reshape(NPAN, BP, NPAN, BP).transpose(0, 2, 1, 3),
        "a_cols": adj.reshape(NPAN, BP, NPAN, BP).transpose(0, 2, 1, 3)[:, :, :, TURNED:],
        "WT": np.asarray(L0_gnn_W).T,
        "b_row": np.asarray(L0_gnn_b),
        "alpha": np.asarray(L0_gnn_alpha),
        "w_par": np.asarray(L1_gnn_w_par), "b_par": np.asarray(L1_gnn_b_par),
        "w_chi": np.asarray(L1_gnn_w_chi), "b_chi": np.asarray(L1_gnn_b_chi),
    }
    arrays = {f"in_{k}": np.ascontiguousarray(v) for k, v in arrays.items()}
    nc = bacc.Bacc("TRN2", target_bir_lowering=False, num_devices=1)
    args = [nc.dram_tensor(k, v.shape, mybir.dt.from_np(v.dtype), kind="ExternalInput").ap() for k, v in arrays.items()]
    out = nc.dram_tensor("out_0", (N, D), F32, kind="ExternalOutput").ap()
    adj_resnorm_kernel(nc, *args, out)
    r = run_bass_kernel_spmd(nc, [arrays], core_ids=[0])
    return r.results[0]["out_0"]
```
